# Optimizing a Trainium2 kernel written in Bass

```python
import numpy as np
import jax
import jax.numpy as jnp

def _softmax(x, axis=-1):
    return jax.nn.softmax(x, axis=axis)

def _gelu(x):
    return jax.nn.gelu(x, approximate=True)

def _silu(x):
    return jax.nn.silu(x)

def _sigmoid(x):
    return jax.nn.sigmoid(x)

def _layernorm(x, axis=-1, eps=1e-05):
    m = jnp.mean(x, axis=axis, keepdims=True)
    v = jnp.var(x, axis=axis, keepdims=True)
    return (x - m) / jnp.sqrt(v + eps)

def _scatter_add(tgt, idx, src, axis=0):
    return tgt.at[idx].add(src)

def _segment_sum(src, seg, n):
    return jax.ops.segment_sum(src, seg, n)
kernel_name = 'mk_seq_postln_d1_jaxref_r8_2afdf5'

def setup_inputs(seed: int=0):
    np.random.seed(seed)
    _w = jnp.asarray

    def _L0_attn_setup():
        import jax, jax.numpy as jnp
        import numpy as np
        WINDOW = 4
        TOPK = 8
        key = jax.random.key(seed)
        ks = jax.random.split(key, 14)
        B, N, D = (4, 256, 128)
        s = 0.02
        w = lambda k_, shp: jax.random.normal(k_, shp, jnp.float32) * s
        return {'mu': jax.random.normal(ks[0], (B, N, D), jnp.float32), 'Wq': w(ks[1], (D, D)), 'bq': jnp.zeros((D,), jnp.float32), 'Wk': w(ks[2], (D, D)), 'bk': jnp.zeros((D,), jnp.float32), 'Wv': w(ks[3], (D, D)), 'bv': jnp.zeros((D,), jnp.float32), 'Wm1': w(ks[4], (2 * D, D)), 'bm1': jnp.zeros((D,), jnp.float32), 'Wm2': w(ks[5], (D, D)), 'bm2': jnp.zeros((D,), jnp.float32), 'Wo': w(ks[6], (2 * D, D)), 'bo': jnp.zeros((D,), jnp.float32)}
    _L0_attn_in = _L0_attn_setup()

    def _L0_ffn_setup():
        import jax, jax.numpy as jnp
        import numpy as np
        DIM = 128
        HIDDEN = 256
        N_EXPERTS = 8
        TOP_K = 2
        EPS = 1e-06

        def rms_norm(x, scale, eps=EPS):
            ms = jnp.mean(jnp.square(x.astype(jnp.float32)), axis=-1, keepdims=True)
            s = scale.astype(jnp.float32) * jax.lax.rsqrt(ms + eps)
            return x * s.astype(x.dtype)

        def moe_linear(xf, ids, W):
            E = W.shape[0]
            out = jnp.zeros((xf.shape[0], W.shape[1]), dtype=xf.dtype)
            for e in range(E):
                out = out + jnp.where((ids == e)[:, None], xf @ W[e].T, 0.0)
            return out
        key = jax.random.key(seed)
        k1, k2, k3, k4 = jax.random.split(key, 4)
        x = jax.random.normal(k1, (4, 512, DIM), dtype=jnp.float32)
        norm_scale = jnp.ones((DIM,), dtype=jnp.float32)
        w_router = jax.random.normal(k2, (N_EXPERTS, DIM), dtype=jnp.float32) / np.sqrt(DIM)
        lim_up = np.sqrt(6.0 / (DIM + 2 * HIDDEN))
        w_up = jax.random.uniform(k3, (N_EXPERTS, 2 * HIDDEN, DIM), dtype=jnp.float32, minval=-lim_up, maxval=lim_up)
        lim_dn = np.sqrt(6.0 / (HIDDEN + DIM))
        w_down = jax.random.uniform(k4, (N_EXPERTS, DIM, HIDDEN), dtype=jnp.float32, minval=-lim_dn, maxval=lim_dn)
        return {'x': x, 'norm_scale': norm_scale, 'w_router': w_router, 'w_up': w_up, 'w_down': w_down}
    _L0_ffn_in = _L0_ffn_setup()
    _d = {'L0_attn_mu': _L0_attn_in['mu'], 'L0_attn_Wq': _L0_attn_in['Wq'], 'L0_attn_bq': _L0_attn_in['bq'], 'L0_attn_Wk': _L0_attn_in['Wk'], 'L0_attn_bk': _L0_attn_in['bk'], 'L0_attn_Wv': _L0_attn_in['Wv'], 'L0_attn_bv': _L0_attn_in['bv'], 'L0_attn_Wm1': _L0_attn_in['Wm1'], 'L0_attn_bm1': _L0_attn_in['bm1'], 'L0_attn_Wm2': _L0_attn_in['Wm2'], 'L0_attn_bm2': _L0_attn_in['bm2'], 'L0_attn_Wo': _L0_attn_in['Wo'], 'L0_attn_bo': _L0_attn_in['bo'], 'L0_ffn_norm_scale': _L0_ffn_in['norm_scale'], 'L0_ffn_w_router': _L0_ffn_in['w_router'], 'L0_ffn_w_up': _L0_ffn_in['w_up'], 'L0_ffn_w_down': _L0_ffn_in['w_down']}
    _x0 = _d['L0_attn_mu']
    _d['L0_attn_mu'] = jax.random.normal(jax.random.fold_in(jax.random.key(seed), 1), (4, 1024, 128), dtype=_x0.dtype)
    del _x0
    return _d

def reference(L0_attn_mu, L0_attn_Wq, L0_attn_bq, L0_attn_Wk, L0_attn_bk, L0_attn_Wv, L0_attn_bv, L0_attn_Wm1, L0_attn_bm1, L0_attn_Wm2, L0_attn_bm2, L0_attn_Wo, L0_attn_bo, L0_ffn_norm_scale, L0_ffn_w_router, L0_ffn_w_up, L0_ffn_w_down):

    def _L0_attn_ref(mu, Wq, bq, Wk, bk, Wv, bv, Wm1, bm1, Wm2, bm2, Wo, bo):
        import jax, jax.numpy as jnp
        import numpy as np
        WINDOW = 4
        TOPK = 8
        B, N, D = mu.shape
        padded = jnp.pad(mu, ((0, 0), (WINDOW, 0), (0, 0)))
        neighbors = jnp.stack([padded[:, WINDOW - w:WINDOW - w + N, :] for w in range(1, WINDOW + 1)], axis=2)
        self_exp = jnp.broadcast_to(mu[:, :, None, :], neighbors.shape)
        h = jnp.concatenate([self_exp, neighbors], axis=-1)
        h = jax.nn.silu(h @ Wm1 + bm1) @ Wm2 + bm2
        local_msgs = h.mean(axis=2)
        q = mu @ Wq + bq
        k = mu @ Wk + bk
        v = mu @ Wv + bv
        scores = jnp.einsum('bnd,bmd->bnm', q, k) / np.sqrt(D).astype(np.float32)
        causal_mask = jnp.triu(jnp.ones((N, N), dtype=bool), k=1)
        scores = jnp.where(causal_mask[None], -jnp.inf, scores)
        if N > TOPK:
            topk_v, topk_i = jax.lax.top_k(scores, TOPK)
            bi = jnp.arange(B)[:, None, None]
            ni = jnp.arange(N)[None, :, None]
            sparse = jnp.full_like(scores, -jnp.inf).at[bi, ni, topk_i].set(topk_v)
            attn = jax.nn.softmax(sparse, axis=-1)
        else:
            attn = jax.nn.softmax(scores, axis=-1)
        glob = jnp.einsum('bnm,bmd->bnd', attn, v)
        return jnp.concatenate([local_msgs, glob], axis=-1) @ Wo + bo

    def _L0_ffn_ref(x, norm_scale, w_router, w_up, w_down):
        import jax, jax.numpy as jnp
        import numpy as np
        DIM = 128
        HIDDEN = 256
        N_EXPERTS = 8
        TOP_K = 2
        EPS = 1e-06

        def rms_norm(x, scale, eps=EPS):
            ms = jnp.mean(jnp.square(x.astype(jnp.float32)), axis=-1, keepdims=True)
            s = scale.astype(jnp.float32) * jax.lax.rsqrt(ms + eps)
            return x * s.astype(x.dtype)

        def moe_linear(xf, ids, W):
            E = W.shape[0]
            out = jnp.zeros((xf.shape[0], W.shape[1]), dtype=xf.dtype)
            for e in range(E):
                out = out + jnp.where((ids == e)[:, None], xf @ W[e].T, 0.0)
            return out
        B, S, D = x.shape
        skip = x
        xn = rms_norm(x, norm_scale)
        scores = (xn @ w_router.T).astype(jnp.float32)
        scores_topk, idx = jax.lax.top_k(scores, TOP_K)
        weights = jax.nn.softmax(scores_topk, axis=-1)
        xf = jnp.broadcast_to(xn[..., None, :], (B, S, TOP_K, D)).reshape(-1, D)
        ids = idx.reshape(-1)
        up = moe_linear(xf, ids, w_up)
        u, gate = jnp.split(up, 2, axis=-1)
        h = u * jax.nn.silu(gate)
        down = moe_linear(h, ids, w_down)
        down = down.reshape(B, S, TOP_K, D)
        out = jnp.sum(down * weights[..., None].astype(down.dtype), axis=-2)
        return out + skip
    x = L0_attn_mu
    x = _layernorm(x + _L0_attn_ref(x, L0_attn_Wq, L0_attn_bq, L0_attn_Wk, L0_attn_bk, L0_attn_Wv, L0_attn_bv, L0_attn_Wm1, L0_attn_bm1, L0_attn_Wm2, L0_attn_bm2, L0_attn_Wo, L0_attn_bo), axis=-1)
    x = _layernorm(x + _L0_ffn_ref(x, L0_ffn_norm_scale, L0_ffn_w_router, L0_ffn_w_up, L0_ffn_w_down), axis=-1)
    return x

_drawn_inputs = setup_inputs


def setup_inputs(seed=0):
    import zlib

    import numpy as np

    out = dict(_drawn_inputs(seed))
    spreads = {'L0_attn_bq': (0.0, 1.269),
     'L0_attn_bk': (0.0, 2.0),
     'L0_attn_bv': (0.0, 0.356),
     'L0_attn_bm1': (0.0, 0.8),
     'L0_attn_bm2': (0.0, 0.367),
     'L0_attn_bo': (0.0, 0.1),
     'L0_ffn_norm_scale': (1.0, 0.2)}
    factors = {'L0_attn_Wm1': 7.197, 'L0_attn_Wm2': 6.308, 'L0_attn_Wq': 3.725, 'L0_attn_Wv': 2.674}
    for name, (base, spread) in spreads.items():
        noise = np.random.default_rng([zlib.crc32(name.encode()), seed]).standard_normal(out[name].shape)
        drawn = base * np.exp(spread * noise) if base else spread * noise
        out[name] = jnp.asarray(drawn.astype(out[name].dtype))
    for name, factor in factors.items():
        out[name] = (out[name] * factor).astype(out[name].dtype)
    return out
```

```python
import numpy as np
import concourse.bass as bass
from concourse import mybir
from contextlib import ExitStack

P = 128
B, N, D = 4, 1024, 128
T = B * N
TILES = T // P
BT = N // P
WINDOW = 4
TOPK = 8
EXPERTS, HIDDEN = 8, 256
CH = 512
CHUNKS = T // CH
CT = CH // P
TURN = 2 * BT
LN_EPS, RMS_EPS = 1e-5, 1e-6
SCALE = float(1.0 / np.sqrt(D))
MASKED = -1e30
TAKEN = -3e38
CAP = T + P
ROW = D + 2
PAIRS = 2 * T
FTILES = PAIRS // P + EXPERTS - 1
RING = 8
NOWHERE = 1 << 20


def build(nc, io):
    F32, BF16 = mybir.dt.float32, mybir.dt.bfloat16
    I32, U32 = mybir.dt.int32, mybir.dt.uint32
    ALU = mybir.AluOpType
    ACT = mybir.ActivationFunctionType
    X = mybir.AxisListType.X

    ctx = ExitStack()
    with ctx:
        def sb(name, shape, dt=F32):
            return ctx.enter_context(nc.sbuf_tensor(name, shape, dt))

        def sem(name):
            return ctx.enter_context(nc.semaphore(name))

        buckets = nc.dram_tensor("buckets", [EXPERTS * CAP, ROW], F32, kind="Internal").ap()
        ydram = nc.dram_tensor("expert_out", [PAIRS, D], F32, kind="Internal").ap()

        wq = sb("wq", [P, D]); wk = sb("wk", [P, D])
        wm1 = sb("wm1", [P, 2, D])
        wo = sb("wo", [P, 2, D])
        wvT = sb("wvT", [P, D]); wm2T = sb("wm2T", [P, D])
        cols = sb("cols", [P, 4])
        reps = sb("reps", [P, 3, P])
        ident = sb("ident", [P, P])
        cbf = sb("cbf", [P, 4, P], BF16)
        ebase = sb("ebase", [P, BT * EXPERTS], BF16)
        iota8 = sb("iota8", [P, EXPERTS])
        dsts = sb("dsts", [P, TILES, 2], I32)
        tiota = sb("tiota", [1, FTILES])
        epsc = sb("epsc", [P, 2])
        wvo = sb("wvo", [P, D]); w2o = sb("w2o", [P, D]); bias_bc = sb("bias_bc", [P, D])
        wr = sb("wr", [P, EXPERTS])
        wup = sb("wup", [P, EXPERTS * 2 * HIDDEN])
        wdn = sb("wdn", [P, EXPERTS * HIDDEN])

        xres = sb("xres", [P, TILES, D])
        qT = sb("qT", [P, T]); kT = sb("kT", [P, T]); vp = sb("vp", [P, TILES * D])

        xTc = sb("xTc", [P, 2, CH])
        cb = sb("cb", [P, WINDOW + N])
        pre = sb("pre", [P, WINDOW, CH]); sil = sb("sil", [P, WINDOW, CH])
        sum2 = sb("sum2", [P, 2, CH]); locT = sb("locT", [P, 2, CH])

        qb = sb("qb", [P, 2, N])
        ex = sb("ex", [P, 2, N])
        pr = sb("pr", [P, 2, N])
        top = sb("top", [P, 2, 8]); nbias = sb("nbias", [P, 2]); e8 = sb("e8", [P, 2, 8])
        lsum = sb("lsum", [P, 2]); rl = sb("rl", [P, 2])
        pT = sb("pT", [P, 2, CH])
        yt = sb("yt", [P, 2, D]); stats = sb("stats", [P, 2, 6]); mv = sb("mv", [P, 2, 2])
        lnv = sb("lnv", [P, 2, 2]); rstd = sb("rstd", [P, 2, 2])
        xnT = sb("xnT", [P, 2, P])
        rows = sb("rows", [P, 2, BT, 2, ROW])
        sc = sb("sc", [P, BT, EXPERTS])
        r8 = sb("r8", [P, BT, 8]); ri = sb("ri", [P, BT, 8], U32)
        idxf = sb("idxf", [P, BT, 2]); oh = sb("oh", [P, 2, BT, EXPERTS])
        chosen = sb("chosen", [P, BT, EXPERTS], BF16)
        count = sb("count", [P, EXPERTS]); countb = sb("countb", [P, EXPERTS], BF16)
        cred = sb("cred", [P, EXPERTS])
        sdif = sb("sdif", [P, BT]); edif = sb("edif", [P, BT]); eden = sb("eden", [P, BT])
        rk = sb("rk", [P, BT * EXPERTS]); rko = sb("rko", [P, 2, BT, EXPERTS])
        posf = sb("posf", [P, 2, BT]); posi = sb("posi", [P, 2, 2, BT], I32)
        total = sb("total", [P, EXPERTS]); ntf = sb("ntf", [1, EXPERTS])
        totali = sb("totali", [1, EXPERTS], I32); nti = sb("nti", [1, EXPERTS], I32)
        zero8 = sb("zero8", [1, EXPERTS]); ends = sb("ends", [1, EXPERTS])
        past = sb("past", [1, FTILES, EXPERTS]); step8 = sb("step8", [1, EXPERTS])
        pstep = sb("pstep", [1, FTILES, EXPERTS])
        tef = sb("tef", [1, FTILES]); rowf = sb("rowf", [1, FTILES]); rowg = sb("rowg", [1, FTILES])
        rowlim = sb("rowlim", [1, 1])
        te = sb("te", [1, FTILES], I32); rowi = sb("rowi", [1, FTILES], I32)
        pad = sb("pad", [P, ROW])
        xg = sb("xg", [P, RING, ROW]); xgT = sb("xgT", [P, 2, P])
        sg = sb("sg", [P, 2, HIDDEN]); hh = sb("hh", [P, 2, HIDDEN]); hT = sb("hT", [P, 2, HIDDEN])
        yo = sb("yo", [P, RING, D])
        ya = qT; yb = kT
        st2 = sb("st2", [P, BT, 6]); mv2 = sb("mv2", [P, BT, 2])
        ln2 = sb("ln2", [P, BT]); rs2 = sb("rs2", [P, BT])

        PS = ctx.enter_context(nc.psum_tensor("PS", [P, 8, 512], F32))
        def score(slot, w):
            return PS[:, 2 * slot:2 * slot + 2, :].rearrange("p a n -> p (a n)")[:, 0:w]

        S_w = sem("weights_loaded"); S_c = sem("constants_loaded"); S_f = sem("ffn_weights_loaded")
        S_x = sem("x_loaded")
        S_xT = [sem("xT_loaded0"), sem("xT_loaded1")]
        S_init = sem("pads_set"); S_fold = sem("weights_folded"); S_foldc = sem("folded_copied")
        S_q = sem("q_made"); S_k = sem("k_made"); S_a = sem("a_made"); S_cc = sem("c_made"); S_v = sem("v_made")
        S_qs = sem("q_stored"); S_ks = sem("k_stored"); S_cs = sem("c_stored"); S_vs = sem("v_stored")
        S_pre = sem("preact_made"); S_sil = sem("silu_made"); S_s2 = sem("silu_pairs_summed")
        S_loc = sem("local_summed"); S_l = sem("local_projected"); S_xb = sem("bias_added")
        S_base = sem("base_made")
        S_qb = [sem("q_staged0"), sem("q_staged1")]
        S_sc = sem("scores_made"); S_top = sem("top8_found"); S_nb = sem("neg_max_made")
        S_ex = sem("exp_made"); S_ls = sem("exp_sum_made"); S_mt = sem("top8_taken"); S_pr = sem("probs_made")
        S_tp = sem("probs_transposed"); S_ts = sem("probs_T_stored"); S_pv = sem("attention_out_made")
        S_pvg = sem("probs_T_used")
        S_rl = sem("recip_sum_made"); S_y = sem("y_made"); S_st = sem("stats_made"); S_mv = sem("mean_var_made")
        S_ln = sem("ln_var_made"); S_rs = sem("rstd_made"); S_x1 = sem("x1_made"); S_xn = sem("xn_made")
        S_xnt = sem("xn_transposed"); S_xns = sem("xn_T_stored"); S_rt = sem("router_made"); S_rts = sem("router_stored")
        S_r8 = sem("router_sorted"); S_ri = sem("router_ranked"); S_id = sem("choice_float"); S_oh = sem("onehot_made")
        S_ch = sem("chosen_made"); S_cr = sem("chosen_counted"); S_ct = sem("count_updated"); S_cb = sem("count_copied")
        S_sd = sem("score_gap_made"); S_ed = sem("exp_gap_made"); S_en = sem("gap_den_made")
        S_w0 = sem("weight0_made"); S_w1 = sem("weight1_made")
        S_rk = sem("rank_made"); S_rks = sem("rank_stored"); S_ro = sem("rank_chosen"); S_pf = sem("position_made")
        S_pi = sem("position_int"); S_ds = sem("dst_written"); S_scat = [sem("scattered0"), sem("scattered1")]
        S_tot = sem("totals_made"); S_tots = sem("totals_stored"); S_tab = sem("table_step"); S_tabd = sem("tables_done")
        S_padv = sem("pad_made"); S_padw = sem("pad_written"); S_wsc = sem("up_scaled"); S_wrs = sem("router_scaled")
        S_g = [sem(f"rows_loaded{i}") for i in range(RING)]
        S_gt = sem("rows_transposed"); S_gs = sem("rows_T_stored"); S_up = sem("gate_made"); S_uu = sem("up_made")
        S_si = sem("gate_silu_made"); S_h = sem("h_made"); S_ht = sem("h_transposed"); S_hs = sem("h_T_stored")
        S_dn = sem("down_made"); S_yo = sem("y_weighted")
        S_ys = [sem(f"y_scattered{i}") for i in range(RING)]
        S_ya = [sem(f"y_fetched{i}") for i in range(B)]
        S_f1 = sem("choices_added"); S_f2 = sem("final_sum_made"); S_f3 = sem("final_stats"); S_f4 = sem("final_mean_var")
        S_f5 = sem("final_ln"); S_f6 = sem("final_rstd"); S_f7 = sem("final_normed"); S_out = sem("out_stored"); S_passed = sem("waits_passed")

        block = ctx.enter_context(nc.Block())
        WLOADS, CLOADS = 9, 7

        def lag(base, u, back):
            return base + max(0, u + 1 - back)

        def settled(engine):
            engine.sem_inc(S_passed, 1)

        GROUPS = [-(-(i + 1) // CT) for i in range(BT)]
        GBEFORE = [sum((GROUPS * 2)[:u]) for u in range(TURN)]
        GTURN = 2 * sum(GROUPS)

        @block.sync
        def _(sp):
            for dst, src in ((wq[:], io["Wq"]), (wk[:], io["Wk"]),
                             (wm1[:], io["Wm1"].rearrange("(a p) n -> p a n", p=P)),
                             (wo[:], io["Wo"].rearrange("(a p) n -> p a n", p=P)),
                             (wvT[:], io["WvT"]), (wm2T[:], io["Wm2T"]),
                             (cols[:], io["cols"]), (reps[:], io["reps"]), (ident[:], io["ident"])):
                sp.dma_start(dst, src).then_inc(S_w, 16)
            with sp.Fori(0, B) as b:
                for h in range(2):
                    sp.wait_ge(S_v, b * 2)
                    sp.dma_start(xTc[:, h, :], io["muT"][:, bass.ds(b * N + h * CH, CH)]).then_inc(S_xT[h], 16)
            with sp.Fori(0, 2) as pair:
                for hb in range(2):
                    sp.wait_ge(S_qs, CHUNKS)
                    sp.wait_ge(S_sc, pair * TURN + hb * BT * 0)
                    sp.dma_start(qb[:, hb, :], qT[:, bass.ds(pair * 2 * N + hb * N, N)]).then_inc(S_qb[hb], 16)
            sp.wait_ge(S_padv, 1)
            sp.wait_ge(S_tabd, 1)
            for e in range(EXPERTS):
                cnt = sp.value_load(totali[0:1, e:e + 1], min_val=0, max_val=T)
                sp.dma_start(buckets[bass.ds(cnt + e * CAP, P), :], pad[:]).then_inc(S_padw, 16)
            sp.wait_ge(S_padw, 16 * EXPERTS)
            for hb in range(2):
                sp.wait_ge(S_scat[hb], 2 * BT * 2 * 16)

            def load_rows(j, r, turn):
                sp.wait_ge(S_ys[r], turn * 16)
                row = sp.value_load(rowi[0:1, bass.ds(j, 1)], min_val=0, max_val=EXPERTS * CAP - P)
                sp.dma_start(xg[:, r, :], buckets[bass.ds(row, P), :]).then_inc(S_g[r], 16)

            with sp.Fori(0, FTILES // RING) as it:
                for r in range(RING):
                    load_rows(it * RING + r, r, it)
            for j in range(FTILES // RING * RING, FTILES):
                load_rows(j, j % RING, j // RING)
            for r in range(RING):
                sp.wait_ge(S_ys[r], 16 * (-(-(FTILES - r) // RING)))
            y0 = ydram[0:T, :].rearrange("(b t p) n -> b p t n", b=B, p=P)
            y1 = ydram[T:2 * T, :].rearrange("(b t p) n -> b p t n", b=B, p=P)
            for b in range(B):
                sp.dma_start(ya[:, b * N:(b + 1) * N].rearrange("p (t n) -> p t n", n=D), y0[b]).then_inc(S_ya[b], 16)
                sp.dma_start(yb[:, b * N:(b + 1) * N].rearrange("p (t n) -> p t n", n=D), y1[b]).then_inc(S_ya[b], 16)
            out = io["out"].rearrange("(b t p) n -> b p t n", b=B, p=P)
            for b in range(B):
                sp.wait_ge(S_f7, b + 1)
                sp.dma_start(out[b], ya[:, b * N:(b + 1) * N].rearrange("p (t n) -> p t n", n=D)).then_inc(S_out, 16)
            sp.wait_ge(S_out, 16 * B)

        @block.tensor
        def _(pe):
            mm = nc.tensor.matmul
            pe.wait_ge(S_w, 16 * WLOADS)
            mm(PS[:, 6, 0:D], wvT[:], wo[:, 1, :], start=True, stop=True)
            mm(PS[:, 6, D:2 * D], wm2T[:], wo[:, 0, :], start=True, stop=True)
            mm(PS[:, 6, 2 * D:3 * D], reps[:, 0, :], wo[:, 0, :], start=True, stop=False)
            mm(PS[:, 6, 2 * D:3 * D], reps[:, 1, :], wo[:, 1, :], start=False, stop=False)
            mm(PS[:, 6, 2 * D:3 * D], ident[:], reps[:, 2, :], start=False, stop=True).then_inc(S_fold, 1)

            def project(c, h, b):
                pe.wait_ge(S_xT[h], b * 16 + 16)
                for bank, w, made, stored in ((0, wq[:], S_q, S_qs), (1, wk[:], S_k, S_ks),
                                              (2, wm1[:, 0, :], S_a, S_pre), (3, wm1[:, 1, :], S_cc, S_cs)):
                    pe.wait_ge(stored, c)
                    mm(PS[:, bank, :], w, xTc[:, h, :], start=True, stop=True).then_inc(made, 1)
                pe.wait_ge(S_vs, c)
                for j in range(CT):
                    last = mm(PS[:, 4, j * D:(j + 1) * D], xTc[:, h, j * P:(j + 1) * P], wvo[:], start=True, stop=True)
                last.then_inc(S_v, 1)

            def local(c, h):
                pe.wait_ge(S_loc, c + 1)
                pe.wait_ge(S_base, c)
                for j in range(CT):
                    last = mm(PS[:, 5, j * D:(j + 1) * D], locT[:, h, j * P:(j + 1) * P], w2o[:], start=True, stop=True)
                last.then_inc(S_l, 1)

            pe.wait_ge(S_foldc, 3)
            project(0, 0, 0)
            with pe.Fori(0, B - 1) as b:
                project(b * 2 + 1, 1, b)
                local(b * 2, 0)
                project(b * 2 + 2, 0, b + 1)
                local(b * 2 + 1, 1)
            project(CHUNKS - 1, 1, B - 1)
            local(CHUNKS - 2, 0)
            local(CHUNKS - 1, 1)

            pe.wait_ge(S_c, 16 * CLOADS)
            pe.wait_ge(S_wrs, 1)
            for s in (S_qs, S_ks, S_pre, S_cs, S_vs, S_base):
                pe.wait_ge(s, CHUNKS)

            with pe.Fori(0, 2) as pair:
                base = pair * TURN
                gbase = pair * GTURN

                def scores(u):
                    hb, i, slot = u // BT, u % BT, u % 2
                    if i == 0:
                        pe.wait_ge(S_qb[hb], pair * 16 + 16)
                    pe.wait_ge(S_ex, lag(base, u, 2))
                    w = (i + 1) * P
                    for c0 in range(0, w, CH):
                        n = min(CH, w - c0)
                        mm(score(slot, w)[:, c0:c0 + n], qb[:, hb, i * P:(i + 1) * P],
                           kT[:, bass.ds(pair * 2 * N + hb * N + c0, n)], start=True, stop=c0 + n < w)
                    mm(score(slot, w)[:, i * P:w], cbf[:, 0, :], cbf[:, 1, :], start=False, stop=True).then_inc(S_sc, 1)

                def attend(u):
                    hb, i, slot = u // BT, u % BT, u % 2
                    pe.wait_ge(S_pr, base + u + 1)
                    ng = GROUPS[i]

                    def turn_probs(g):
                        gg = GBEFORE[u] + g
                        pe.wait_ge(S_ts, lag(gbase, gg, 2))
                        ks = range(g * CT, min((g + 1) * CT, i + 1))
                        for m in ks:
                            last = nc.tensor.transpose(PS[:, 4 + gg % 2, (m - g * CT) * P:(m - g * CT + 1) * P],
                                                       pr[:, slot, m * P:(m + 1) * P], ident[:])
                        last.then_inc(S_tp, 1)

                    def weigh(g):
                        gg = GBEFORE[u] + g
                        pe.wait_ge(S_ts, gbase + gg + 1)
                        if g == 0:
                            pe.wait_ge(S_y, lag(base, u, 1))
                        for m in range(g * CT, min((g + 1) * CT, i + 1)):
                            last = mm(PS[:, 6, 0:D], pT[:, gg % 2, (m - g * CT) * P:(m - g * CT + 1) * P],
                                      vp[:, bass.ds(pair * 2 * N + hb * N + m * D, D)], start=m == 0, stop=m == i)
                        last.then_inc(S_pvg, 1)
                        return last

                    for g in range(ng):
                        turn_probs(g)
                    for g in range(ng):
                        last = weigh(g)

                def turn_xn(u):
                    pe.wait_ge(S_xn, base + u + 1)
                    pe.wait_ge(S_rts, lag(base, u, 1))
                    if u == 0:
                        pe.wait_ge(S_rks, pair * 2)
                    nc.tensor.transpose(PS[:, 7, 0:P], rows[:, u // BT, u % BT, 0, 0:D], ident[:]).then_inc(S_xnt, 1)

                def route(u):
                    pe.wait_ge(S_xns, base + u + 1)
                    if u == BT + 3:
                        pe.wait_ge(S_rks, pair * 2 + 1)
                    mm(PS[:, 7, P:P + EXPERTS], xnT[:, u % 2, :], wr[:], start=True, stop=True).then_inc(S_rt, 1)

                def rank(hb, turned):
                    pe.wait_ge(S_rts, base + (hb + 1) * BT)
                    pe.wait_ge(S_xns, base + turned)
                    pe.wait_ge(S_cb, pair * 2 + hb)
                    pe.wait_ge(S_ch, pair * 2 + hb + 1)
                    r = PS[:, 7, 2 * P:2 * P + BT * EXPERTS]
                    mm(r, cbf[:, 2, :], chosen[:].rearrange("p t e -> p (t e)"), start=True, stop=False)
                    mm(r, cbf[:, 0, :], ebase[:], start=False, stop=False)
                    for j in range(BT - 1):
                        k = BT - 1 - j
                        mm(r[:, (j + 1) * EXPERTS:], cbf[:, 3, :], chosen[:, j:j + 1, :].broadcast_to([P, k, EXPERTS]),
                           start=False, stop=False, skip_group_check=True)
                    mm(r, cbf[:, 3, :], countb[:].unsqueeze(1).broadcast_to([P, BT, EXPERTS]),
                       start=False, stop=True).then_inc(S_rk, 1)

                scores(0)
                scores(1)
                for u in range(TURN):
                    attend(u)
                    if u + 2 < TURN:
                        scores(u + 2)
                    if u >= 3:
                        route(u - 3)
                    if u >= 2:
                        turn_xn(u - 2)
                    if u == BT + 5:
                        rank(0, BT + 4)
                route(TURN - 3)
                turn_xn(TURN - 2)
                route(TURN - 2)
                turn_xn(TURN - 1)
                route(TURN - 1)
                rank(1, TURN)

            pe.wait_ge(S_cb, B)
            pe.wait_ge(S_rks, B)
            mm(PS[:, 7, 0:EXPERTS], cbf[:, 3, :], countb[:], start=True, stop=True).then_inc(S_tot, 1)

            pe.wait_ge(S_f, 32)
            pe.wait_ge(S_wsc, 1)
            pe.wait_ge(S_tots, 1)
            pe.wait_ge(S_tabd, 1)

            def turn_rows(j, r, t16):
                pe.wait_ge(S_g[r % RING], t16)
                if not (isinstance(j, int) and j == 0):
                    pe.wait_ge(S_gs, j)
                nc.tensor.transpose(PS[:, 0, 0:P], xg[:, r % RING, 0:D], ident[:]).then_inc(S_gt, 1)

            def expert(j):
                return pe.value_load(te[0:1, bass.ds(j, 1)], min_val=0, max_val=EXPERTS - 1)

            def gate(j, r, e):
                pe.wait_ge(S_gs, j + 1)
                pe.wait_ge(S_si, j)
                mm(PS[:, 1, 0:HIDDEN], xgT[:, r % 2, :], wup[:, bass.ds(e * (2 * HIDDEN) + HIDDEN, HIDDEN)],
                   start=True, stop=True).then_inc(S_up, 1)

            def up(j, r, e):
                pe.wait_ge(S_h, j)
                mm(PS[:, 2, 0:HIDDEN], xgT[:, r % 2, :], wup[:, bass.ds(e * (2 * HIDDEN), HIDDEN)],
                   start=True, stop=True).then_inc(S_uu, 1)

            def turn_h(j, r):
                pe.wait_ge(S_h, j + 1)
                pe.wait_ge(S_hs, j)
                for k in range(2):
                    last = nc.tensor.transpose(PS[:, 3, k * P:(k + 1) * P], hh[:, r % 2, k * P:(k + 1) * P], ident[:])
                last.then_inc(S_ht, 1)

            def down(j, r, e):
                pe.wait_ge(S_hs, j + 1)
                pe.wait_ge(S_yo, j)
                for k in range(2):
                    last = mm(PS[:, 4, 0:D], hT[:, r % 2, k * P:(k + 1) * P],
                              wdn[:, bass.ds(e * HIDDEN + k * D, D)], start=k == 0, stop=k == 1)
                last.then_inc(S_dn, 1)

            turn_rows(0, 0, 16)
            turn_rows(1, 1, 16)
            e0 = expert(0)
            gate(0, 0, e0)
            up(0, 0, e0)

            def tile(j, r, turn, more1, more2):
                if more2:
                    turn_rows(j + 2, r + 2, turn * 16 + (16 if r + 2 < RING else 32))
                if more1:
                    en = expert(j + 1)
                    gate(j + 1, r + 1, en)
                turn_h(j, r)
                if more1:
                    up(j + 1, r + 1, en)
                down(j, r, expert(j))

            with pe.Fori(0, FTILES // RING) as it:
                for r in range(RING):
                    tile(it * RING + r, r, it, True, True)
            for j in range(FTILES // RING * RING, FTILES):
                tile(j, j % RING, j // RING, j + 1 < FTILES, j + 2 < FTILES)

        @block.scalar
        def _(act):
            ac = nc.scalar.activation
            for dst, src in ((cbf[:], io["cbf"]), (ebase[:], io["ebase"]), (iota8[:], io["iota8"]),
                             (dsts[:], io["dsts"]), (tiota[:], io["tiota"]), (epsc[:], io["epsc"]),
                             (wr[:], io["wrT"])):
                act.dma_start(dst, src).then_inc(S_c, 16)
            act.wait_ge(S_w, 16 * WLOADS)
            act.wait_ge(S_fold, 1)
            ac(wvo[:], PS[:, 6, 0:D], ACT.Copy).then_inc(S_foldc, 1)
            ac(w2o[:], PS[:, 6, D:2 * D], ACT.Copy, scale=1.0 / WINDOW).then_inc(S_foldc, 1)
            ac(bias_bc[:], PS[:, 6, 2 * D:3 * D], ACT.Copy).then_inc(S_foldc, 1)
            ac(cb[:, 0:WINDOW], PS[:, 6, 0:WINDOW], ACT.Identity, bias=cols[:, 2:3], scale=0.0).then_inc(S_init, 1)

            with act.Fori(0, B) as b:
                for h in range(2):
                    c = b * 2 + h
                    act.wait_ge(S_q, c + 1)
                    ac(qT[:, bass.ds(b * N + h * CH, CH)], PS[:, 0, :], ACT.Identity, bias=cols[:, 0:1]).then_inc(S_qs, 1)
                    act.wait_ge(S_cc, c + 1)
                    act.wait_ge(S_pre, c)
                    ac(cb[:, WINDOW + h * CH:WINDOW + (h + 1) * CH], PS[:, 3, :], ACT.Identity,
                       bias=cols[:, 2:3]).then_inc(S_cs, 1)
                    act.wait_ge(S_k, c + 1)
                    ac(kT[:, bass.ds(b * N + h * CH, CH)], PS[:, 1, :], ACT.Identity, bias=cols[:, 1:2]).then_inc(S_ks, 1)
                    act.wait_ge(S_pre, c + 1)
                    act.wait_ge(S_loc, c)
                    ac(sil[:], pre[:], ACT.Silu).then_inc(S_sil, 1)

            act.wait_ge(S_c, 16 * CLOADS)
            with act.Fori(0, 2) as pair:
                base = pair * TURN
                gbase = pair * GTURN

                def exps(u):
                    w, slot = (u % BT + 1) * P, u % 2
                    act.wait_ge(S_mt, base + u + 1)
                    act.wait_ge(S_pr, lag(base, u, 2))
                    ac(ex[:, slot, 0:w], score(slot, w), ACT.Exp, bias=nbias[:, slot:slot + 1], scale=SCALE).then_inc(S_ex, 1)
                    act.wait_ge(S_rl, lag(base, u, 2))
                    ac(e8[:, slot, :], top[:, slot, :], ACT.Exp, bias=nbias[:, slot:slot + 1], scale=SCALE,
                       accum_out=lsum[:, slot:slot + 1]).then_inc(S_ls, 1)

                def store_probs(u):
                    i = u % BT
                    for g in range(GROUPS[i]):
                        gg = GBEFORE[u] + g
                        n = min(CT, i + 1 - g * CT) * P
                        act.wait_ge(S_tp, gbase + gg + 1)
                        act.wait_ge(S_pvg, lag(gbase, gg, 2))
                        ac(pT[:, gg % 2, 0:n], PS[:, 4 + gg % 2, 0:n], ACT.Copy).then_inc(S_ts, 1)

                def rstds(u):
                    s = u % 2
                    act.wait_ge(S_mv, base + u + 1)
                    act.wait_ge(S_xn, lag(base, u, 2))
                    ac(lnv[:, s, 0:1], mv[:, s, 1:2], ACT.Ln, bias=epsc[:, 0:1])
                    ac(lnv[:, s, 1:2], mv[:, s, 1:2], ACT.Ln, bias=epsc[:, 1:2], scale=1.0 + RMS_EPS).then_inc(S_ln, 1)
                    act.wait_ge(S_ln, base + u + 1)
                    ac(rstd[:, s, :], lnv[:, s, :], ACT.Exp, scale=-0.5).then_inc(S_rs, 1)

                def store_xn(u):
                    act.wait_ge(S_xnt, base + u + 1)
                    act.wait_ge(S_rt, lag(base, u, 2))
                    ac(xnT[:, u % 2, :], PS[:, 7, 0:P], ACT.Copy).then_inc(S_xns, 1)

                def store_route(u):
                    act.wait_ge(S_rt, base + u + 1)
                    if u % BT == 0:
                        act.wait_ge(S_sd, pair * 2 + u // BT)
                        act.wait_ge(S_ri, pair * 2 + u // BT)
                    ac(sc[:, u % BT, :], PS[:, 7, P:P + EXPERTS], ACT.Copy).then_inc(S_rts, 1)

                def gap(hb):
                    act.wait_ge(S_sd, pair * 2 + hb + 1)
                    act.wait_ge(S_w1, pair * 2 + hb)
                    ac(edif[:], sdif[:], ACT.Exp).then_inc(S_ed, 1)

                def store_rank(hb):
                    act.wait_ge(S_rk, pair * 2 + hb + 1)
                    act.wait_ge(S_ro, pair * 2 + hb)
                    ac(rk[:], PS[:, 7, 2 * P:2 * P + BT * EXPERTS], ACT.Copy).then_inc(S_rks, 1)

                exps(0)
                for u in range(TURN):
                    store_probs(u)
                    if u + 1 < TURN:
                        exps(u + 1)
                    if u >= 3:
                        store_route(u - 3)
                    if u >= 2:
                        store_xn(u - 2)
                    if u >= 1:
                        rstds(u - 1)
                    if u == BT + 3:
                        gap(0)
                    if u == BT + 5:
                        store_rank(0)
                store_route(TURN - 3)
                store_xn(TURN - 2)
                rstds(TURN - 1)
                store_route(TURN - 2)
                store_xn(TURN - 1)
                store_route(TURN - 1)
                gap(1)
                store_rank(1)

            act.wait_ge(S_tot, 1)
            ac(total[:], PS[:, 7, 0:EXPERTS], ACT.Copy).then_inc(S_tots, 1)

            def store_rows(j, r):
                act.wait_ge(S_gt, j + 1)
                ac(xgT[:, r % 2, :], PS[:, 0, 0:P], ACT.Copy).then_inc(S_gs, 1)

            def silu(j, r):
                act.wait_ge(S_up, j + 1)
                ac(sg[:, r % 2, :], PS[:, 1, 0:HIDDEN], ACT.Silu).then_inc(S_si, 1)

            def store_h(j, r):
                act.wait_ge(S_ht, j + 1)
                ac(hT[:, r % 2, :], PS[:, 3, 0:HIDDEN], ACT.Copy).then_inc(S_hs, 1)

            store_rows(0, 0)
            store_rows(1, 1)
            silu(0, 0)

            def tile(j, r, more1, more2):
                if more2:
                    act.wait_ge(S_uu, j + 1)
                    store_rows(j + 2, r + 2)
                if more1:
                    silu(j + 1, r + 1)
                store_h(j, r)

            with act.Fori(0, FTILES // RING) as it:
                for r in range(RING):
                    tile(it * RING + r, r, True, True)
            for j in range(FTILES // RING * RING, FTILES):
                tile(j, j % RING, j + 1 < FTILES, j + 2 < FTILES)
            for b in range(B):
                act.wait_ge(S_f4, b + 1)
                ac(ln2[:], mv2[:, :, 1], ACT.Ln, bias=epsc[:, 0:1]).then_inc(S_f5, 1)
                act.wait_ge(S_f5, b + 1)
                ac(rs2[:], ln2[:], ACT.Exp, scale=-0.5).then_inc(S_f6, 1)

        @block.vector
        def _(dve):
            ve = nc.vector
            ts, tt, stt = ve.tensor_scalar, ve.tensor_tensor, ve.scalar_tensor_tensor
            ve.memset(count[:], 0.0)
            ve.memset(zero8[:], 0.0)
            ve.memset(pad[:, 0:D], 0.0)
            ve.memset(pad[:, D:D + 1].bitcast(I32), NOWHERE)
            ve.memset(pad[:, D + 1:ROW], 0.0).then_inc(S_padv, 1)
            ve.memset(countb[:], 0.0)
            dve.wait_ge(S_init, 1)

            def preact(c, h):
                dve.wait_ge(S_a, c + 1)
                dve.wait_ge(S_cs, c + 1)
                dve.wait_ge(S_sil, c)
                a = PS[:, 2, :].unsqueeze(1).broadcast_to([P, WINDOW, CH])
                full = cb[:]
                near = bass.AP(tensor=full.tensor, offset=full.offset + h * CH,
                               ap=[full.ap[0], [1, WINDOW], [1, CH]])
                tt(pre[:], a, near, ALU.add).then_inc(S_pre, 1)

            def basis(c, b, h):
                dve.wait_ge(S_l, c + 1)
                dve.wait_ge(S_xb, B)
                v = xres[:, bass.ds(b * BT + h * CT, CT), :].rearrange("p t n -> p (t n)")
                tt(v, PS[:, 5, :], v, ALU.add).then_inc(S_base, 1)

            def store_v(c, b, h):
                dve.wait_ge(S_v, c + 1)
                ve.tensor_copy(vp[:, bass.ds(b * N + h * CH, CH)], PS[:, 4, :]).then_inc(S_vs, 1)

            preact(0, 0)
            store_v(0, 0, 0)
            with dve.Fori(0, B - 1) as b:
                preact(b * 2 + 1, 1)
                store_v(b * 2 + 1, b, 1)
                basis(b * 2, b, 0)
                preact(b * 2 + 2, 0)
                store_v(b * 2 + 2, b + 1, 0)
                basis(b * 2 + 1, b, 1)
            preact(CHUNKS - 1, 1)
            store_v(CHUNKS - 1, B - 1, 1)
            basis(CHUNKS - 2, B - 1, 0)
            basis(CHUNKS - 1, B - 1, 1)

            dve.wait_ge(S_c, 16 * CLOADS)
            dve.wait_ge(S_base, CHUNKS)
            with dve.Fori(0, 2) as pair:
                base = pair * TURN

                def top8(u):
                    w, s = (u % BT + 1) * P, u % 2
                    dve.wait_ge(S_sc, base + u + 1)
                    dve.wait_ge(S_ls, lag(base, u, 2))
                    settled(dve)
                    ve.max(top[:, s, :], score(s, w)).then_inc(S_top, 1)
                    dve.wait_ge(S_top, base + u + 1)
                    ts(nbias[:, s:s + 1], top[:, s, 0:1], -SCALE, None, ALU.mult).then_inc(S_nb, 1)
                    dve.wait_ge(S_tp, pair * GTURN + (GBEFORE[u - 1] if u >= 2 else 0))
                    settled(dve)
                    ve.match_replace(pr[:, s, 0:w], top[:, s, :], score(s, w), TAKEN).then_inc(S_mt, 1)

                def probs(u):
                    w, s = (u % BT + 1) * P, u % 2
                    dve.wait_ge(S_mt, base + u + 1)
                    dve.wait_ge(S_ex, base + u + 1)
                    stt(pr[:, s, 0:w], pr[:, s, 0:w], TAKEN / 2, ex[:, s, 0:w], ALU.is_lt, ALU.mult).then_inc(S_pr, 1)

                def first_norm(u):
                    s = u % 2
                    dve.wait_ge(S_ls, base + u + 1)
                    ve.reciprocal(rl[:, s:s + 1], lsum[:, s:s + 1]).then_inc(S_rl, 1)
                    dve.wait_ge(S_rl, base + u + 1)
                    dve.wait_ge(S_pvg, pair * GTURN + GBEFORE[u] + GROUPS[u % BT])
                    stt(yt[:, s, :], PS[:, 6, 0:D], rl[:, s:s + 1],
                        xres[:, bass.ds(base + u, 1), :].rearrange("p a n -> p (a n)"), ALU.mult, ALU.add).then_inc(S_y, 1)
                    dve.wait_ge(S_y, base + u + 1)
                    ve.bn_stats(stats[:, s, :], yt[:, s, :]).then_inc(S_st, 1)
                    dve.wait_ge(S_st, base + u + 1)
                    settled(dve)
                    ve.bn_aggr(mv[:, s, :], stats[:, s, :]).then_inc(S_mv, 1)

                def normed(u):
                    s, hb, i = u % 2, u // BT, u % BT
                    dve.wait_ge(S_rs, base + u + 1)
                    if i == 0:
                        dve.wait_ge(S_scat[hb], pair * (2 * BT * 16))
                    ts(rows[:, hb, i, :, 0:D], yt[:, s, :].unsqueeze(1).broadcast_to([P, 2, D]),
                       mv[:, s, 0:1], rstd[:, s, 1:2], ALU.subtract, ALU.mult).then_inc(S_xn, 1)
                    ts(xres[:, bass.ds(base + u, 1), :].rearrange("p a n -> p (a n)"), yt[:, s, :],
                       mv[:, s, 0:1], rstd[:, s, 0:1], ALU.subtract, ALU.mult).then_inc(S_x1, 1)

                def choose(hb):
                    n = pair * 2 + hb
                    dve.wait_ge(S_rts, base + (hb + 1) * BT)
                    settled(dve)
                    for i in range(BT):
                        last = ve.max(r8[:, i, :], sc[:, i, :])
                    last.then_inc(S_r8, 1)
                    dve.wait_ge(S_r8, n + 1)
                    settled(dve)
                    for i in range(BT):
                        last = ve.max_index(ri[:, i, :], r8[:, i, :], sc[:, i, :])
                    last.then_inc(S_ri, 1)
                    tt(sdif[:], r8[:, :, 1], r8[:, :, 0], ALU.subtract).then_inc(S_sd, 1)
                    dve.wait_ge(S_ri, n + 1)
                    ve.tensor_copy(idxf[:], ri[:, :, 0:2]).then_inc(S_id, 1)
                    dve.wait_ge(S_id, n + 1)
                    for k in range(2):
                        last = tt(oh[:, k], iota8[:].unsqueeze(1).broadcast_to([P, BT, EXPERTS]),
                                  idxf[:, :, k:k + 1].broadcast_to([P, BT, EXPERTS]), ALU.is_equal)
                    last.then_inc(S_oh, 1)
                    dve.wait_ge(S_oh, n + 1)
                    tt(chosen[:], oh[:, 0], oh[:, 1], ALU.add).then_inc(S_ch, 1)
                    dve.wait_ge(S_ed, n + 1)
                    ts(eden[:], edif[:], 1.0, None, ALU.add).then_inc(S_en, 1)
                    dve.wait_ge(S_en, n + 1)
                    ve.reciprocal(rows[:, hb, :, 0, D + 1], eden[:]).then_inc(S_w0, 1)
                    dve.wait_ge(S_w0, n + 1)
                    tt(rows[:, hb, :, 1, D + 1], edif[:], rows[:, hb, :, 0, D + 1], ALU.mult).then_inc(S_w1, 1)

                def place(hb):
                    n = pair * 2 + hb
                    dve.wait_ge(S_rks, n + 1)
                    dve.wait_ge(S_ch, n + 1)
                    ve.tensor_reduce(cred[:], chosen[:].rearrange("p t e -> p e t"), X, ALU.add).then_inc(S_cr, 1)
                    dve.wait_ge(S_cr, n + 1)
                    tt(count[:], count[:], cred[:], ALU.add).then_inc(S_ct, 1)
                    dve.wait_ge(S_ct, n + 1)
                    ve.tensor_copy(countb[:], count[:]).then_inc(S_cb, 1)
                    tt(rko[:], oh[:], rk[:].rearrange("p (t e) -> p t e", e=EXPERTS).unsqueeze(1).broadcast_to([P, 2, BT, EXPERTS]),
                       ALU.mult).then_inc(S_ro, 1)
                    dve.wait_ge(S_ro, n + 1)
                    ve.tensor_reduce(posf[:], rko[:], X, ALU.add).then_inc(S_pf, 1)
                    dve.wait_ge(S_pf, n + 1)
                    dve.wait_ge(S_scat[hb], pair * (2 * BT * 16))
                    ve.tensor_copy(posi[:, hb], posf[:]).then_inc(S_pi, 1)

                top8(0)
                for u in range(TURN):
                    if u + 1 < TURN:
                        top8(u + 1)
                    probs(u)
                    if u >= 2:
                        normed(u - 2)
                    if u >= 1:
                        first_norm(u - 1)
                    if u == BT + 3:
                        choose(0)
                    if u == BT + 5:
                        place(0)
                normed(TURN - 2)
                first_norm(TURN - 1)
                normed(TURN - 1)
                choose(1)
                place(1)

            def step(k, ins):
                ins.then_inc(S_tab, 1)
                dve.wait_ge(S_tab, k)

            dve.wait_ge(S_tots, 1)
            step(1, ts(ntf[:], total[0:1, :], float(P - 1), None, ALU.add))
            step(2, ve.tensor_copy(nti[:], ntf[:]))
            step(3, ve.tensor_copy(totali[:], total[0:1, :]))
            step(4, ts(nti[:], nti[:], 7, None, ALU.arith_shift_right))
            step(5, ve.tensor_copy(ntf[:], nti[:]))
            step(6, ve.tensor_tensor_scan(ends[:], ntf[:], zero8[:], 0.0, ALU.add, ALU.add))
            step(7, tt(past[:], tiota[:].unsqueeze(2).broadcast_to([1, FTILES, EXPERTS]),
                       ends[:].unsqueeze(1).broadcast_to([1, FTILES, EXPERTS]), ALU.is_ge))
            step(8, ts(step8[:], ntf[:], -float(P), float(CAP), ALU.mult, ALU.add))
            step(9, ve.tensor_reduce(tef[:], past[:, :, 0:EXPERTS - 1], X, ALU.add))
            step(10, tt(pstep[:], past[:], step8[:].unsqueeze(1).broadcast_to([1, FTILES, EXPERTS]), ALU.mult))
            step(11, ve.tensor_reduce(rowf[:], pstep[:, :, 0:EXPERTS - 1], X, ALU.add))
            step(12, stt(rowg[:], tiota[:], float(P), rowf[:], ALU.mult, ALU.add))
            step(13, ts(rowlim[:], total[0:1, EXPERTS - 1:EXPERTS], float((EXPERTS - 1) * CAP), None, ALU.add))
            step(14, ts(rowi[:], rowg[:], rowlim[:], None, ALU.min))
            step(15, ve.tensor_copy(te[:], tef[:]))
            ve.tensor_copy(zero8[:], ends[:]).then_inc(S_tabd, 1)

            def hidden(j, r):
                dve.wait_ge(S_si, j + 1)
                dve.wait_ge(S_uu, j + 1)
                tt(hh[:, r % 2, :], PS[:, 2, 0:HIDDEN], sg[:, r % 2, :], ALU.mult).then_inc(S_h, 1)

            def weighted(j, r, turn):
                dve.wait_ge(S_dn, j + 1)
                dve.wait_ge(S_ys[r], turn * 16)
                ts(yo[:, r, :], PS[:, 4, 0:D], xg[:, r, D + 1:ROW], None, ALU.mult).then_inc(S_yo, 1)

            hidden(0, 0)

            def tile(j, r, turn, more):
                if more:
                    hidden(j + 1, r + 1)
                weighted(j, r, turn)

            with dve.Fori(0, FTILES // RING) as it:
                for r in range(RING):
                    tile(it * RING + r, r, it, True)
            for j in range(FTILES // RING * RING, FTILES):
                tile(j, j % RING, j // RING, j + 1 < FTILES)

            for b in range(B):
                a, c = ya[:, b * N:(b + 1) * N], yb[:, b * N:(b + 1) * N]
                dve.wait_ge(S_ya[b], 32)
                tt(a, a, c, ALU.add).then_inc(S_f1, 1)
                dve.wait_ge(S_f1, b + 1)
                stt(c, xres[:, b * BT:(b + 1) * BT, :].rearrange("p t n -> p (t n)"), 2.0, a, ALU.mult, ALU.add).then_inc(S_f2, 1)
                dve.wait_ge(S_f2, b + 1)
                for i in range(BT):
                    last = ve.bn_stats(st2[:, i, :], c[:, i * D:(i + 1) * D])
                last.then_inc(S_f3, 1)
                dve.wait_ge(S_f3, b + 1)
                if b:
                    dve.wait_ge(S_f7, b)
                for i in range(BT):
                    last = ve.bn_aggr(mv2[:, i, :], st2[:, i, :])
                last.then_inc(S_f4, 1)
                dve.wait_ge(S_f6, b + 1)
                for i in range(BT):
                    last = ts(a[:, i * D:(i + 1) * D], c[:, i * D:(i + 1) * D], mv2[:, i, 0:1], rs2[:, i:i + 1],
                              ALU.subtract, ALU.mult)
                last.then_inc(S_f7, 1)

        @block.gpsimd
        def _(pool):
            gp = nc.gpsimd
            gp.dma_start(xres[:], io["mu"].rearrange("(t p) n -> p t n", p=P)).then_inc(S_x, 16)
            gp.dma_start(wup[:], io["wupT"]).then_inc(S_f, 16)
            gp.dma_start(wdn[:], io["wdnT"]).then_inc(S_f, 16)

            def add_bias(b):
                v = xres[:, b * BT:(b + 1) * BT, :]
                gp.tensor_tensor(v, v, bias_bc[:].unsqueeze(1).broadcast_to([P, BT, D]), ALU.add).then_inc(S_xb, 1)

            def sum_window(c, h, projected):
                pool.wait_ge(S_sil, c + 1)
                gp.tensor_tensor(sum2[:], sil[:, 0:2, :], sil[:, 2:4, :], ALU.add).then_inc(S_s2, 1)
                pool.wait_ge(S_s2, c + 1)
                pool.wait_ge(S_l, projected)
                gp.tensor_tensor(locT[:, h, :], sum2[:, 0, :], sum2[:, 1, :], ALU.add).then_inc(S_loc, 1)

            pool.wait_ge(S_x, 16)
            pool.wait_ge(S_foldc, 3)
            for b in range(B):
                add_bias(b)
            sum_window(0, 0, 0)
            with pool.Fori(0, B - 1) as b:
                sum_window(b * 2 + 1, 1, b * 2)
                sum_window(b * 2 + 2, 0, b * 2 + 1)
            sum_window(CHUNKS - 1, 1, CHUNKS - 2)
            pool.wait_ge(S_f, 32)
            pool.wait_ge(S_w, 16 * WLOADS)
            pool.wait_ge(S_c, 16 * CLOADS)
            gp.tensor_scalar(wr[:], wr[:], cols[:, 3:4], 1.0, ALU.mult, ALU.mult).then_inc(S_wrs, 1)
            gp.tensor_scalar(wup[:], wup[:], cols[:, 3:4], 1.0, ALU.mult, ALU.mult).then_inc(S_wsc, 1)

            pool.wait_ge(S_c, 16 * CLOADS)
            with pool.Fori(0, 2) as pair:
                for hb in range(2):
                    n = pair * 2 + hb
                    pool.wait_ge(S_scat[hb], pair * (2 * BT * 16))
                    gp.tensor_copy(rows[:, hb, :, :, D:D + 1].bitcast(I32).rearrange("p t k o -> p t (k o)"),
                                   dsts[:, bass.ds(n * BT, BT), :]).then_inc(S_ds, 1)
                    pool.wait_ge(S_ds, n + 1)
                    pool.wait_ge(S_pi, n + 1)
                    pool.wait_ge(S_w1, n + 1)
                    pool.wait_ge(S_xn, n * BT + BT)
                    settled(pool)
                    for i in range(BT):
                        for k in range(2):
                            gp.indirect_dma_start(
                                buckets, bass.IndirectOffsetOnAxis(ap=posi[:, hb, k, i:i + 1], axis=0),
                                rows[:, hb, i, k, :], None).then_inc(S_scat[hb], 16)

            def scatter(j, r):
                pool.wait_ge(S_yo, j + 1)
                settled(pool)
                gp.indirect_dma_start(
                    ydram, bass.IndirectOffsetOnAxis(ap=xg[:, r, D:D + 1].bitcast(I32), axis=0),
                    yo[:, r, :], None, bounds_check=PAIRS - 1, oob_is_err=False).then_inc(S_ys[r], 16)

            with pool.Fori(0, FTILES // RING) as it:
                for r in range(RING):
                    scatter(it * RING + r, r)
            for j in range(FTILES // RING * RING, FTILES):
                scatter(j, j % RING)


def kernel(**inputs):
    import ml_dtypes
    import concourse.bacc as bacc
    from concourse.bass_utils import run_bass_kernel_spmd

    g = {k.replace("L0_attn_", "").replace("L0_ffn_", ""): np.asarray(v) for k, v in inputs.items()}
    c = np.ascontiguousarray
    mu = g["mu"].reshape(T, D)
    arrays = {
        "mu": c(mu), "muT": c(mu.T), "Wq": c(g["Wq"]), "Wk": c(g["Wk"]), "Wm1": c(g["Wm1"]), "Wo": c(g["Wo"]),
        "WvT": c(g["Wv"].T), "Wm2T": c(g["Wm2"].T),
        "cols": c(np.stack([g["bq"], g["bk"], g["bm1"], g["norm_scale"]], axis=1)),
        "reps": c(np.stack([np.broadcast_to(g["bm2"][:, None], (D, P)), np.broadcast_to(g["bv"][:, None], (D, P)),
                            np.broadcast_to(g["bo"][None, :], (P, D))], axis=1)),
        "wrT": c(g["w_router"].T),
        "wupT": c(g["w_up"].transpose(2, 0, 1).reshape(D, EXPERTS * 2 * HIDDEN)),
        "wdnT": c(g["w_down"].transpose(2, 0, 1).reshape(2, P, EXPERTS, D).transpose(1, 2, 0, 3).reshape(P, EXPERTS * HIDDEN)),
    }
    r = np.arange(P)
    arrays["ident"] = np.eye(P, dtype=np.float32)
    arrays["cbf"] = np.stack([np.eye(P), np.where(r[None, :] > r[:, None], MASKED, 0.0),
                              r[:, None] < r[None, :], np.ones((P, P))], axis=1).astype(ml_dtypes.bfloat16)
    arrays["ebase"] = np.broadcast_to(np.tile(np.arange(EXPERTS) * CAP, BT), (P, BT * EXPERTS)).astype(ml_dtypes.bfloat16)
    arrays["iota8"] = np.broadcast_to(np.arange(EXPERTS, dtype=np.float32), (P, EXPERTS)).copy()
    arrays["dsts"] = (r[:, None, None] + np.arange(TILES)[None, :, None] * P + np.arange(2)[None, None, :] * T).astype(np.int32)
    arrays["tiota"] = np.arange(FTILES, dtype=np.float32)[None, :]
    arrays["epsc"] = np.broadcast_to(np.array([LN_EPS, RMS_EPS * LN_EPS], np.float32), (P, 2)).copy()

    nc = bacc.Bacc("TRN2", target_bir_lowering=False, num_devices=1)
    io = {k: nc.dram_tensor(f"in_{k}", a.shape, mybir.dt.from_np(a.dtype), kind="ExternalInput").ap() for k, a in arrays.items()}
    io["out"] = nc.dram_tensor("out", [T, D], mybir.dt.float32, kind="ExternalOutput").ap()
    build(nc, io)
    res = run_bass_kernel_spmd(nc, [{f"in_{k}": a for k, a in arrays.items()}], core_ids=[0])
    return res.results[0]["out"].reshape(B, N, D)
```

```python
import numpy as np
import concourse.bass as bass
from concourse import mybir
from contextlib import ExitStack

P = 128
B, N, D = 4, 1024, 128
T = B * N
TILES = T // P
BT = N // P
WINDOW = 4
TOPK = 8
EXPERTS, HIDDEN = 8, 256
CH = 512
CHUNKS = T // CH
CT = CH // P
G = 4
NG = TILES // G
LN_EPS, RMS_EPS = 1e-5, 1e-6
SCALE = float(1.0 / np.sqrt(D))
MASKED = -1e30
TAKEN = -3e38
CAP = T + P
ROW = D + 2
PAIRS = 2 * T
FTILES = PAIRS // P + EXPERTS - 1
RING = 8
NOWHERE = 1 << 20


ORDER = ([(0, i) for i in range(BT)]
         + [(s, i) for k in range(BT) for s, i in ((1, BT - 1 - k), (2, k))]
         + [(3, BT - 1 - i) for i in range(BT)])


def build(nc, io):
    F32, BF16 = mybir.dt.float32, mybir.dt.bfloat16
    I32, U32 = mybir.dt.int32, mybir.dt.uint32
    ALU = mybir.AluOpType
    ACT = mybir.ActivationFunctionType
    X = mybir.AxisListType.X

    ctx = ExitStack()
    with ctx:
        def sb(name, shape, dt=F32):
            return ctx.enter_context(nc.sbuf_tensor(name, shape, dt))

        def sem(name):
            return ctx.enter_context(nc.semaphore(name))

        buckets = nc.dram_tensor("buckets", [EXPERTS * CAP, ROW], F32, kind="Internal").ap()
        ydram = nc.dram_tensor("expert_out", [PAIRS, D], F32, kind="Internal").ap()

        wq = sb("wq", [P, D]); wk = sb("wk", [P, D])
        wm1 = sb("wm1", [P, 2, D])
        wo = sb("wo", [P, 2, D])
        wvT = sb("wvT", [P, D]); wm2T = sb("wm2T", [P, D])
        cols = sb("cols", [P, 4])
        reps = sb("reps", [P, 3, P])
        ident = sb("ident", [P, P])
        cbf = sb("cbf", [P, 4, P], BF16)
        ebase = sb("ebase", [P, G * EXPERTS], BF16)
        iota8 = sb("iota8", [P, EXPERTS])
        dsts = sb("dsts", [P, TILES, 2], I32)
        tiota = sb("tiota", [1, FTILES])
        epsc = sb("epsc", [P, 2])
        wvo = sb("wvo", [P, D]); w2o = sb("w2o", [P, D]); bias_bc = sb("bias_bc", [P, D])
        wr = sb("wr", [P, EXPERTS])
        wup = sb("wup", [P, EXPERTS * 2 * HIDDEN])
        wdn = sb("wdn", [P, EXPERTS * HIDDEN])

        xres = sb("xres", [P, TILES, D])
        qT = sb("qT", [P, T]); kT = sb("kT", [P, T]); vp = sb("vp", [P, TILES * D])

        xTc = sb("xTc", [P, 2, CH])
        cb = sb("cb", [P, WINDOW + N])
        pre = sb("pre", [P, WINDOW, CH]); sil = sb("sil", [P, WINDOW, CH])
        sum2 = sb("sum2", [P, 2, CH]); locT = sb("locT", [P, 2, CH])

        ex = sb("ex", [P, 2, N])
        pr = sb("pr", [P, 2, N])
        top = sb("top", [P, 2, 8]); nbias = sb("nbias", [P, 2]); e8 = sb("e8", [P, 2, 8])
        lsum = sb("lsum", [P, 2]); rl = sb("rl", [P, 2])
        pT = sb("pT", [P, 2, CH])
        stats = sb("stats", [P, 2, 6])
        mv = sb("mv", [P, 2, G, 2]); vv = sb("vv", [P, G, 2]); lnv = sb("lnv", [P, G, 2])
        r0 = sb("r0", [P, G, 2]); rsq = sb("rsq", [P, G, 2]); rh = sb("rh", [P, G, 2])
        rstd = sb("rstd", [P, 2, G, 2])
        xnT = sb("xnT", [P, G * P])
        rows = sb("rows", [P, 2, G, 2, ROW])
        sc = sb("sc", [P, G, EXPERTS])
        r8 = sb("r8", [P, G, 8]); ri = sb("ri", [P, G, 8], U32)
        idxf = sb("idxf", [P, G, 2]); oh = sb("oh", [P, 2, G, EXPERTS])
        chosen = sb("chosen", [P, G, EXPERTS], BF16)
        count = sb("count", [P, EXPERTS]); countb = sb("countb", [P, EXPERTS], BF16)
        cred = sb("cred", [P, EXPERTS])
        sdif = sb("sdif", [P, G]); edif = sb("edif", [P, G]); eden = sb("eden", [P, G])
        rk = sb("rk", [P, G * EXPERTS]); rko = sb("rko", [P, 2, G, EXPERTS])
        posf = sb("posf", [P, 2, G]); posi = sb("posi", [P, 2, 2, G], I32)
        total = sb("total", [P, EXPERTS]); ntf = sb("ntf", [1, EXPERTS])
        totali = sb("totali", [1, EXPERTS], I32); nti = sb("nti", [1, EXPERTS], I32)
        zero8 = sb("zero8", [1, EXPERTS]); ends = sb("ends", [1, EXPERTS])
        past = sb("past", [1, FTILES, EXPERTS]); step8 = sb("step8", [1, EXPERTS])
        pstep = sb("pstep", [1, FTILES, EXPERTS])
        tef = sb("tef", [1, FTILES]); rowf = sb("rowf", [1, FTILES]); rowg = sb("rowg", [1, FTILES])
        rowlim = sb("rowlim", [1, 1])
        te = sb("te", [1, FTILES], I32); rowi = sb("rowi", [1, FTILES], I32)
        pad = sb("pad", [P, ROW])
        xg = sb("xg", [P, RING, ROW]); xgT = sb("xgT", [P, 2, P])
        sg = sb("sg", [P, 2, HIDDEN]); hh = sb("hh", [P, 2, HIDDEN]); hT = sb("hT", [P, 2, HIDDEN])
        yo = sb("yo", [P, RING, D])
        ya = qT; yb = kT
        st2 = sb("st2", [P, 2, G, 6]); mv2 = sb("mv2", [P, 2, G, 2])
        vv2 = sb("vv2", [P, 2, G]); ln2 = sb("ln2", [P, 2, G]); r02 = sb("r02", [P, 2, G])
        rq2 = sb("rq2", [P, 2, G]); rh2 = sb("rh2", [P, 2, G]); rs2 = sb("rs2", [P, 2, G])

        PS = ctx.enter_context(nc.psum_tensor("PS", [P, 8, 512], F32))
        def score(slot, w):
            return PS[:, 2 * slot:2 * slot + 2, :].rearrange("p a n -> p (a n)")[:, 0:w]

        S_w = sem("weights_loaded"); S_c = sem("constants_loaded"); S_f = sem("ffn_weights_loaded")
        S_x = sem("x_loaded")
        S_xT = [sem("xT_loaded0"), sem("xT_loaded1")]
        S_init = sem("pads_set"); S_fold = sem("weights_folded"); S_foldc = sem("folded_copied")
        S_q = sem("q_made"); S_k = sem("k_made"); S_a = sem("a_made"); S_cc = sem("c_made"); S_v = sem("v_made")
        S_qs = sem("q_stored"); S_ks = sem("k_stored"); S_cs = sem("c_stored"); S_vs = sem("v_stored")
        S_pre = sem("preact_made"); S_sil = sem("silu_made"); S_s2 = sem("silu_pairs_summed")
        S_loc = sem("local_summed"); S_l = sem("local_projected"); S_xb = sem("bias_added")
        S_base = sem("base_made")
        S_sc = sem("scores_made"); S_top = sem("top8_found"); S_nb = sem("neg_max_made")
        S_ex = sem("exp_made"); S_ls = sem("exp_sum_made"); S_mt = sem("top8_taken"); S_pr = sem("probs_made")
        S_tp = sem("probs_transposed"); S_ts = sem("probs_T_stored"); S_pv = sem("attention_out_made")
        S_pvg = sem("probs_T_used")
        S_rl = sem("recip_sum_made"); S_y = sem("y_made"); S_st = sem("stats_made"); S_mv = sem("mean_var_made")
        S_ln = sem("ln_var_made"); S_rs = sem("rstd_made"); S_x1 = sem("x1_made"); S_xn = sem("xn_made")
        S_xnt = sem("xn_transposed"); S_xns = sem("xn_T_stored"); S_rt = sem("router_made"); S_rts = sem("router_stored")
        S_r8 = sem("router_sorted"); S_ri = sem("router_ranked"); S_id = sem("choice_float"); S_oh = sem("onehot_made")
        S_ch = sem("chosen_made"); S_cr = sem("chosen_counted"); S_ct = sem("count_updated"); S_cb = sem("count_copied")
        S_sd = sem("score_gap_made"); S_ed = sem("exp_gap_made"); S_en = sem("gap_den_made")
        S_w0 = sem("weight0_made"); S_w1 = sem("weight1_made")
        S_rk = sem("rank_made"); S_rks = sem("rank_stored"); S_ro = sem("rank_chosen"); S_pf = sem("position_made")
        S_pi = sem("position_int"); S_ds = sem("dst_written"); S_scat = [sem("scattered0"), sem("scattered1")]
        S_tot = sem("totals_made"); S_tots = sem("totals_stored"); S_tab = sem("table_step"); S_tabd = sem("tables_done")
        S_padv = sem("pad_made"); S_padw = sem("pad_written"); S_wsc = sem("up_scaled"); S_wrs = sem("router_scaled")
        S_g = [sem(f"rows_loaded{i}") for i in range(RING)]
        S_gt = sem("rows_transposed"); S_gs = sem("rows_T_stored"); S_up = sem("gate_made"); S_uu = sem("up_made")
        S_si = sem("gate_silu_made"); S_h = sem("h_made"); S_ht = sem("h_transposed"); S_hs = sem("h_T_stored")
        S_dn = sem("down_made"); S_yo = sem("y_weighted")
        S_ys = [sem(f"y_scattered{i}") for i in range(RING)]
        S_ya = [sem(f"y_fetched{i}") for i in range(NG)]
        S_f1 = sem("choices_added"); S_f2 = sem("final_sum_made"); S_f3 = sem("final_stats"); S_f4 = sem("final_mean_var")
        S_vv = sem("variance_biased"); S_n1 = sem("rstd_squared"); S_n2 = sem("rstd_error_made"); S_n3 = sem("rstd_refined")
        S_l2 = sem("final_vars"); S_m1 = sem("final_rstd_squared"); S_m2 = sem("final_rstd_error"); S_m3 = sem("final_rstd_refined")
        S_f5 = sem("final_ln"); S_f6 = sem("final_rstd"); S_f7 = sem("final_normed"); S_out = sem("out_stored"); S_passed = sem("waits_passed")

        block = ctx.enter_context(nc.Block())
        WLOADS, CLOADS = 9, 7

        def group(u, back):
            g, r = divmod(u - back, G)
            return g if r == 0 and 0 <= g < NG else None

        def settled(engine):
            engine.sem_inc(S_passed, 1)

        W = [(i + 1) * P for _, i in ORDER]
        STEPS = TILES + 9
        QUADS = [-(-w // CH) for w in W]
        QUADS_BEFORE = [sum(QUADS[:u]) for u in range(TILES + 1)]
        ALLSCAT = NG // 2 * G * 2 * 16

        @block.sync
        def _(sp):
            for dst, src in ((wq[:], io["Wq"]), (wk[:], io["Wk"]),
                             (wm1[:], io["Wm1"].rearrange("(a p) n -> p a n", p=P)),
                             (wo[:], io["Wo"].rearrange("(a p) n -> p a n", p=P)),
                             (wvT[:], io["WvT"]), (wm2T[:], io["Wm2T"]),
                             (cols[:], io["cols"]), (reps[:], io["reps"]), (ident[:], io["ident"])):
                sp.dma_start(dst, src).then_inc(S_w, 16)
            with sp.Fori(0, B) as b:
                for h in range(2):
                    sp.wait_ge(S_v, b * 2)
                    sp.dma_start(xTc[:, h, :], io["muT"][:, bass.ds(b * N + h * CH, CH)]).then_inc(S_xT[h], 16)
            sp.dma_start(wup[:], io["wupT"]).then_inc(S_f, 16)
            sp.dma_start(wdn[:], io["wdnT"]).then_inc(S_f, 16)
            sp.wait_ge(S_padv, 1)
            sp.wait_ge(S_tabd, 1)
            for e in range(EXPERTS):
                cnt = sp.value_load(totali[0:1, e:e + 1], min_val=0, max_val=T)
                sp.dma_start(buckets[bass.ds(cnt + e * CAP, P), :], pad[:]).then_inc(S_padw, 16)
            sp.wait_ge(S_padw, 16 * EXPERTS)
            for hb in range(2):
                sp.wait_ge(S_scat[hb], ALLSCAT)

            def load_rows(j, r, turn):
                sp.wait_ge(S_ys[r], turn * 16)
                row = sp.value_load(rowi[0:1, bass.ds(j, 1)], min_val=0, max_val=EXPERTS * CAP - P)
                sp.dma_start(xg[:, r, :], buckets[bass.ds(row, P), :]).then_inc(S_g[r], 16)

            with sp.Fori(0, FTILES // RING) as it:
                for r in range(RING):
                    load_rows(it * RING + r, r, it)
            for j in range(FTILES // RING * RING, FTILES):
                load_rows(j, j % RING, j // RING)
            for r in range(RING):
                sp.wait_ge(S_ys[r], 16 * (-(-(FTILES - r) // RING)))
            y0 = ydram[0:T, :].rearrange("(g t p) n -> g p t n", t=G, p=P)
            y1 = ydram[T:2 * T, :].rearrange("(g t p) n -> g p t n", t=G, p=P)
            for g in range(NG):
                sp.dma_start(ya[:, g * CH:(g + 1) * CH].rearrange("p (t n) -> p t n", n=D), y0[g]).then_inc(S_ya[g], 16)
                sp.dma_start(yb[:, g * CH:(g + 1) * CH].rearrange("p (t n) -> p t n", n=D), y1[g]).then_inc(S_ya[g], 16)
            out = io["out"].rearrange("(g t p) n -> g p t n", t=G, p=P)
            for g in range(NG):
                sp.wait_ge(S_f7, g + 1)
                sp.dma_start(out[g], ya[:, g * CH:(g + 1) * CH].rearrange("p (t n) -> p t n", n=D)).then_inc(S_out, 16)
            sp.wait_ge(S_out, 16 * NG)

        @block.tensor
        def _(pe):
            mm = nc.tensor.matmul
            pe.wait_ge(S_w, 16 * WLOADS)
            mm(PS[:, 6, 0:D], wvT[:], wo[:, 1, :], start=True, stop=True)
            mm(PS[:, 6, D:2 * D], wm2T[:], wo[:, 0, :], start=True, stop=True)
            mm(PS[:, 6, 2 * D:3 * D], reps[:, 0, :], wo[:, 0, :], start=True, stop=False)
            mm(PS[:, 6, 2 * D:3 * D], reps[:, 1, :], wo[:, 1, :], start=False, stop=False)
            mm(PS[:, 6, 2 * D:3 * D], ident[:], reps[:, 2, :], start=False, stop=True).then_inc(S_fold, 1)

            def project(c, h, b):
                pe.wait_ge(S_xT[h], b * 16 + 16)
                for bank, w, made, stored in ((0, wq[:], S_q, S_qs), (1, wk[:], S_k, S_ks),
                                              (2, wm1[:, 0, :], S_a, S_pre), (3, wm1[:, 1, :], S_cc, S_cs)):
                    pe.wait_ge(stored, c)
                    mm(PS[:, bank, :], w, xTc[:, h, :], start=True, stop=True).then_inc(made, 1)
                pe.wait_ge(S_vs, c)
                for j in range(CT):
                    last = mm(PS[:, 4, j * D:(j + 1) * D], xTc[:, h, j * P:(j + 1) * P], wvo[:], start=True, stop=True)
                last.then_inc(S_v, 1)

            def local(c, h):
                pe.wait_ge(S_loc, c + 1)
                pe.wait_ge(S_base, c)
                for j in range(CT):
                    last = mm(PS[:, 5, j * D:(j + 1) * D], locT[:, h, j * P:(j + 1) * P], w2o[:], start=True, stop=True)
                last.then_inc(S_l, 1)

            pe.wait_ge(S_foldc, 3)
            project(0, 0, 0)
            with pe.Fori(0, B - 1) as b:
                project(b * 2 + 1, 1, b)
                local(b * 2, 0)
                project(b * 2 + 2, 0, b + 1)
                local(b * 2 + 1, 1)
            project(CHUNKS - 1, 1, B - 1)
            local(CHUNKS - 2, 0)
            local(CHUNKS - 1, 1)

            pe.wait_ge(S_c, 16 * CLOADS)
            pe.wait_ge(S_wrs, 1)
            for s in (S_qs, S_ks, S_pre, S_cs, S_vs, S_base):
                pe.wait_ge(s, CHUNKS)

            def scores(u):
                (seq, i), w = ORDER[u], W[u]
                if u >= 2:
                    pe.wait_ge(S_ex, u - 1)
                for c0 in range(0, w, CH):
                    n = min(CH, w - c0)
                    mm(score(u % 2, w)[:, c0:c0 + n], qT[:, seq * N + i * P:seq * N + i * P + P],
                       kT[:, seq * N + c0:seq * N + c0 + n], start=True, stop=c0 + n < w)
                mm(score(u % 2, w)[:, i * P:w], cbf[:, 0, :], cbf[:, 1, :], start=False, stop=True).then_inc(S_sc, 1)

            def attend(u):
                (seq, i), slot = ORDER[u], u % 2
                pe.wait_ge(S_pr, u + 1)
                for g in range(QUADS[u]):
                    q = QUADS_BEFORE[u] + g
                    if q >= 2:
                        pe.wait_ge(S_ts, q - 1)
                    for m in range(g * CT, min((g + 1) * CT, i + 1)):
                        last = nc.tensor.transpose(PS[:, 4 + q % 2, (m - g * CT) * P:(m - g * CT + 1) * P],
                                                   pr[:, slot, m * P:(m + 1) * P], ident[:])
                    last.then_inc(S_tp, 1)
                for g in range(QUADS[u]):
                    q = QUADS_BEFORE[u] + g
                    pe.wait_ge(S_ts, q + 1)
                    if g == 0 and u >= 1:
                        pe.wait_ge(S_y, u)
                    for m in range(g * CT, min((g + 1) * CT, i + 1)):
                        last = mm(PS[:, 6, 0:D], pT[:, q % 2, (m - g * CT) * P:(m - g * CT + 1) * P],
                                  vp[:, seq * N + m * D:seq * N + (m + 1) * D], start=m == 0, stop=m == i)
                    last.then_inc(S_pv, 1)

            def turn_xn(g):
                pe.wait_ge(S_xn, (g + 1) * G)
                if g >= 1:
                    pe.wait_ge(S_rks, g)
                for t in range(G):
                    last = nc.tensor.transpose(PS[:, 7, t * P:(t + 1) * P], rows[:, g % 2, t, 0, 0:D], ident[:])
                last.then_inc(S_xnt, 1)

            def route(g):
                pe.wait_ge(S_xns, g + 1)
                for t in range(G):
                    last = mm(PS[:, 7, t * EXPERTS:(t + 1) * EXPERTS], xnT[:, t * P:(t + 1) * P], wr[:], start=True, stop=True)
                last.then_inc(S_rt, 1)

            def rank(g):
                pe.wait_ge(S_rts, g + 1)
                pe.wait_ge(S_ch, g + 1)
                if g >= 1:
                    pe.wait_ge(S_cb, g + 1)
                r = PS[:, 7, 0:G * EXPERTS]
                mm(r, cbf[:, 2, :], chosen[:].rearrange("p t e -> p (t e)"), start=True, stop=False)
                mm(r, cbf[:, 0, :], ebase[:], start=False, stop=False)
                for j in range(G - 1):
                    k = G - 1 - j
                    mm(r[:, (j + 1) * EXPERTS:], cbf[:, 3, :], chosen[:, j:j + 1, :].broadcast_to([P, k, EXPERTS]),
                       start=False, stop=False, skip_group_check=True)
                mm(r, cbf[:, 3, :], countb[:].unsqueeze(1).broadcast_to([P, G, EXPERTS]),
                   start=False, stop=True).then_inc(S_rk, 1)

            pe.wait_ge(S_cb, 1)
            scores(0)
            scores(1)
            for u in range(STEPS):
                if u + 2 < TILES:
                    scores(u + 2)
                if u < TILES:
                    attend(u)
                if (g := group(u, 7)) is not None:
                    turn_xn(g)
                if (g := group(u, 8)) is not None:
                    route(g)
                if (g := group(u, 10)) is not None:
                    rank(g)

            pe.wait_ge(S_cb, NG + 1)
            pe.wait_ge(S_rks, NG)
            mm(PS[:, 7, 0:EXPERTS], cbf[:, 3, :], countb[:], start=True, stop=True).then_inc(S_tot, 1)

            pe.wait_ge(S_f, 32)
            pe.wait_ge(S_wsc, 1)
            pe.wait_ge(S_tots, 1)
            pe.wait_ge(S_tabd, 1)

            def turn_rows(j, r, t16):
                pe.wait_ge(S_g[r % RING], t16)
                if not (isinstance(j, int) and j == 0):
                    pe.wait_ge(S_gs, j)
                nc.tensor.transpose(PS[:, 0, 0:P], xg[:, r % RING, 0:D], ident[:]).then_inc(S_gt, 1)

            def experts(j, n):
                return nc.values_load_multi_w_load_instructions(
                    te[0:1, bass.ds(j, n)], engines=(mybir.EngineType.PE,), min_val=0, max_val=EXPERTS - 1)[1]

            def gate(j, r, e):
                pe.wait_ge(S_gs, j + 1)
                pe.wait_ge(S_si, j)
                mm(PS[:, 1, 0:HIDDEN], xgT[:, r % 2, :], wup[:, bass.ds(e * (2 * HIDDEN) + HIDDEN, HIDDEN)],
                   start=True, stop=True).then_inc(S_up, 1)

            def up(j, r, e):
                pe.wait_ge(S_h, j)
                mm(PS[:, 2, 0:HIDDEN], xgT[:, r % 2, :], wup[:, bass.ds(e * (2 * HIDDEN), HIDDEN)],
                   start=True, stop=True).then_inc(S_uu, 1)

            def turn_h(j, r):
                pe.wait_ge(S_h, j + 1)
                pe.wait_ge(S_hs, j)
                for k in range(2):
                    last = nc.tensor.transpose(PS[:, 3, k * P:(k + 1) * P], hh[:, r % 2, k * P:(k + 1) * P], ident[:])
                last.then_inc(S_ht, 1)

            def down(j, r, e):
                pe.wait_ge(S_hs, j + 1)
                pe.wait_ge(S_yo, j)
                for k in range(2):
                    last = mm(PS[:, 4, 0:D], hT[:, r % 2, k * P:(k + 1) * P],
                              wdn[:, bass.ds(e * HIDDEN + k * D, D)], start=k == 0, stop=k == 1)
                last.then_inc(S_dn, 1)

            turn_rows(0, 0, 16)
            turn_rows(1, 1, 16)
            e0 = pe.value_load(te[0:1, 0:1], min_val=0, max_val=EXPERTS - 1)
            gate(0, 0, e0)
            up(0, 0, e0)

            def tile(j, r, turn, e, en, more2):
                if more2:
                    turn_rows(j + 2, r + 2, turn * 16 + (16 if r + 2 < RING else 32))
                if en is not None:
                    gate(j + 1, r + 1, en)
                turn_h(j, r)
                if en is not None:
                    up(j + 1, r + 1, en)
                down(j, r, e)

            with pe.Fori(0, FTILES // RING) as it:
                e = experts(it * RING, RING + 1)
                for r in range(RING):
                    tile(it * RING + r, r, it, e[r], e[r + 1], True)
            whole = FTILES // RING * RING
            e = [*experts(whole, FTILES - whole), None]
            for j in range(whole, FTILES):
                tile(j, j % RING, j // RING, e[j - whole], e[j - whole + 1], j + 2 < FTILES)

        @block.scalar
        def _(act):
            ac = nc.scalar.activation
            for dst, src in ((cbf[:], io["cbf"]), (ebase[:], io["ebase"]), (iota8[:], io["iota8"]),
                             (dsts[:], io["dsts"]), (tiota[:], io["tiota"]), (epsc[:], io["epsc"]),
                             (wr[:], io["wrT"])):
                act.dma_start(dst, src).then_inc(S_c, 16)
            act.wait_ge(S_w, 16 * WLOADS)
            act.wait_ge(S_fold, 1)
            ac(wvo[:], PS[:, 6, 0:D], ACT.Copy).then_inc(S_foldc, 1)
            ac(w2o[:], PS[:, 6, D:2 * D], ACT.Copy, scale=1.0 / WINDOW).then_inc(S_foldc, 1)
            ac(bias_bc[:], PS[:, 6, 2 * D:3 * D], ACT.Copy).then_inc(S_foldc, 1)
            ac(cb[:, 0:WINDOW], PS[:, 6, 0:WINDOW], ACT.Identity, bias=cols[:, 2:3], scale=0.0).then_inc(S_init, 1)

            nc.scalar.preload_act_table(ACT.Silu)
            with act.Fori(0, B) as b:
                for h in range(2):
                    c = b * 2 + h
                    act.wait_ge(S_q, c + 1)
                    ac(qT[:, bass.ds(b * N + h * CH, CH)], PS[:, 0, :], ACT.Identity, bias=cols[:, 0:1]).then_inc(S_qs, 1)
                    act.wait_ge(S_cc, c + 1)
                    act.wait_ge(S_pre, c)
                    ac(cb[:, WINDOW + h * CH:WINDOW + (h + 1) * CH], PS[:, 3, :], ACT.Identity,
                       bias=cols[:, 2:3]).then_inc(S_cs, 1)
                    act.wait_ge(S_k, c + 1)
                    ac(kT[:, bass.ds(b * N + h * CH, CH)], PS[:, 1, :], ACT.Identity, bias=cols[:, 1:2]).then_inc(S_ks, 1)
                    act.wait_ge(S_pre, c + 1)
                    act.wait_ge(S_loc, c)
                    ac(sil[:], pre[:], ACT.Silu).then_inc(S_sil, 1)

            nc.scalar.preload_act_table_set("natural_log_exp_and_others")
            act.wait_ge(S_c, 16 * CLOADS)
            def exps(u):
                w, slot = W[u], u % 2
                act.wait_ge(S_nb, u + 1)
                if u >= 2:
                    act.wait_ge(S_pr, u - 1)
                ac(ex[:, slot, 0:w], score(slot, w), ACT.Exp, bias=nbias[:, slot:slot + 1], scale=SCALE).then_inc(S_ex, 1)
                if u >= 2:
                    act.wait_ge(S_rl, u - 1)
                ac(e8[:, slot, :], top[:, slot, :], ACT.Exp, bias=nbias[:, slot:slot + 1], scale=SCALE,
                   accum_out=lsum[:, slot:slot + 1]).then_inc(S_ls, 1)

            def store_probs(u):
                for g in range(QUADS[u]):
                    q = QUADS_BEFORE[u] + g
                    n = min(CH, W[u] - g * CH)
                    act.wait_ge(S_tp, q + 1)
                    if q >= 2:
                        act.wait_ge(S_pv, q - 1)
                    ac(pT[:, q % 2, 0:n], PS[:, 4 + q % 2, 0:n], ACT.Copy).then_inc(S_ts, 1)

            def first_rstd(g):
                act.wait_ge(S_vv, g + 1)
                ac(lnv[:], vv[:], ACT.Ln).then_inc(S_ln, 1)
                act.wait_ge(S_ln, g + 1)
                ac(r0[:], lnv[:], ACT.Exp, scale=-0.5).then_inc(S_rs, 1)

            def store_xn(g):
                act.wait_ge(S_xnt, g + 1)
                ac(xnT[:], PS[:, 7, :], ACT.Copy).then_inc(S_xns, 1)

            def store_route(g):
                act.wait_ge(S_rt, g + 1)
                if g >= 1:
                    act.wait_ge(S_ri, g)
                ac(sc[:], PS[:, 7, 0:G * EXPERTS].rearrange("p (t e) -> p t e", e=EXPERTS), ACT.Copy).then_inc(S_rts, 1)

            def gap(g):
                act.wait_ge(S_sd, g + 1)
                if g >= 1:
                    act.wait_ge(S_w1, g)
                ac(edif[:], sdif[:], ACT.Exp).then_inc(S_ed, 1)

            def store_rank(g):
                act.wait_ge(S_rk, g + 1)
                if g >= 1:
                    act.wait_ge(S_ro, g)
                ac(rk[:], PS[:, 7, 0:G * EXPERTS], ACT.Copy).then_inc(S_rks, 1)

            exps(0)
            for u in range(STEPS):
                if u + 1 < TILES:
                    exps(u + 1)
                if u < TILES:
                    store_probs(u)
                if (g := group(u, 5)) is not None:
                    first_rstd(g)
                if (g := group(u, 7)) is not None:
                    store_xn(g)
                if (g := group(u, 8)) is not None:
                    store_route(g)
                if (g := group(u, 9)) is not None:
                    gap(g)
                if (g := group(u, 10)) is not None:
                    store_rank(g)

            act.wait_ge(S_tot, 1)
            ac(total[:], PS[:, 7, 0:EXPERTS], ACT.Copy).then_inc(S_tots, 1)

            def store_rows(j, r):
                act.wait_ge(S_gt, j + 1)
                ac(xgT[:, r % 2, :], PS[:, 0, 0:P], ACT.Copy).then_inc(S_gs, 1)

            def silu(j, r):
                act.wait_ge(S_up, j + 1)
                ac(sg[:, r % 2, :], PS[:, 1, 0:HIDDEN], ACT.Silu).then_inc(S_si, 1)

            def store_h(j, r):
                act.wait_ge(S_ht, j + 1)
                ac(hT[:, r % 2, :], PS[:, 3, 0:HIDDEN], ACT.Copy).then_inc(S_hs, 1)

            nc.scalar.preload_act_table(ACT.Silu)
            store_rows(0, 0)
            store_rows(1, 1)
            silu(0, 0)

            def tile(j, r, more1, more2):
                if more2:
                    act.wait_ge(S_uu, j + 1)
                    store_rows(j + 2, r + 2)
                if more1:
                    silu(j + 1, r + 1)
                store_h(j, r)

            with act.Fori(0, FTILES // RING) as it:
                for r in range(RING):
                    tile(it * RING + r, r, True, True)
            for j in range(FTILES // RING * RING, FTILES):
                tile(j, j % RING, j + 1 < FTILES, j + 2 < FTILES)
            nc.scalar.preload_act_table_set("natural_log_exp_and_others")
            for g in range(NG):
                act.wait_ge(S_l2, g + 1)
                ac(ln2[:, g % 2, :], vv2[:, g % 2, :], ACT.Ln).then_inc(S_f5, 1)
                act.wait_ge(S_f5, g + 1)
                ac(r02[:, g % 2, :], ln2[:, g % 2, :], ACT.Exp, scale=-0.5).then_inc(S_f6, 1)

        @block.vector
        def _(dve):
            ve = nc.vector
            ts, tt, stt = ve.tensor_scalar, ve.tensor_tensor, ve.scalar_tensor_tensor
            ve.memset(count[:], 0.0)
            ve.memset(zero8[:], 0.0)
            ve.memset(pad[:, 0:D], 0.0)
            ve.memset(pad[:, D:D + 1].bitcast(I32), NOWHERE)
            ve.memset(pad[:, D + 1:ROW], 0.0).then_inc(S_padv, 1)
            ve.memset(countb[:], 0.0).then_inc(S_cb, 1)
            dve.wait_ge(S_init, 1)

            def preact(c, h):
                dve.wait_ge(S_a, c + 1)
                dve.wait_ge(S_cs, c + 1)
                dve.wait_ge(S_sil, c)
                a = PS[:, 2, :].unsqueeze(1).broadcast_to([P, WINDOW, CH])
                full = cb[:]
                near = bass.AP(tensor=full.tensor, offset=full.offset + h * CH,
                               ap=[full.ap[0], [1, WINDOW], [1, CH]])
                tt(pre[:], a, near, ALU.add).then_inc(S_pre, 1)

            def basis(c, b, h):
                dve.wait_ge(S_l, c + 1)
                dve.wait_ge(S_xb, B)
                v = xres[:, bass.ds(b * BT + h * CT, CT), :].rearrange("p t n -> p (t n)")
                tt(v, PS[:, 5, :], v, ALU.add).then_inc(S_base, 1)

            def store_v(c, b, h):
                dve.wait_ge(S_v, c + 1)
                ve.tensor_copy(vp[:, bass.ds(b * N + h * CH, CH)], PS[:, 4, :]).then_inc(S_vs, 1)

            preact(0, 0)
            store_v(0, 0, 0)
            with dve.Fori(0, B - 1) as b:
                preact(b * 2 + 1, 1)
                store_v(b * 2 + 1, b, 1)
                basis(b * 2, b, 0)
                preact(b * 2 + 2, 0)
                store_v(b * 2 + 2, b + 1, 0)
                basis(b * 2 + 1, b, 1)
            preact(CHUNKS - 1, 1)
            store_v(CHUNKS - 1, B - 1, 1)
            basis(CHUNKS - 2, B - 1, 0)
            basis(CHUNKS - 1, B - 1, 1)

            dve.wait_ge(S_c, 16 * CLOADS)
            dve.wait_ge(S_base, CHUNKS)
            def top8(u):
                s = u % 2
                dve.wait_ge(S_sc, u + 1)
                if u >= 2:
                    dve.wait_ge(S_ls, u - 1)
                ve.max(top[:, s, :], score(s, W[u])).then_inc(S_top, 1)

            def take8(u):
                s = u % 2
                dve.wait_ge(S_top, u + 1)
                if u >= 2:
                    dve.wait_ge(S_tp, QUADS_BEFORE[u - 1])
                ve.match_replace(pr[:, s, 0:W[u]], top[:, s, :], score(s, W[u]), TAKEN).then_inc(S_mt, 1)
                ts(nbias[:, s:s + 1], top[:, s, 0:1], -SCALE, None, ALU.mult).then_inc(S_nb, 1)

            def probs(u):
                w, s = W[u], u % 2
                dve.wait_ge(S_mt, u + 1)
                dve.wait_ge(S_ex, u + 1)
                stt(pr[:, s, 0:w], pr[:, s, 0:w], TAKEN / 2, ex[:, s, 0:w], ALU.is_lt, ALU.mult).then_inc(S_pr, 1)

            def recip_sum(u):
                dve.wait_ge(S_ls, u + 1)
                ve.reciprocal(rl[:, u % 2:u % 2 + 1], lsum[:, u % 2:u % 2 + 1]).then_inc(S_rl, 1)

            def tile_of(u):
                return ORDER[u][0] * BT + ORDER[u][1]

            def residual(u):
                dve.wait_ge(S_rl, u + 1)
                dve.wait_ge(S_pv, QUADS_BEFORE[u + 1])
                stt(xres[:, tile_of(u), :], PS[:, 6, 0:D], rl[:, u % 2:u % 2 + 1], xres[:, tile_of(u), :],
                    ALU.mult, ALU.add).then_inc(S_y, 1)

            def tile_stats(u):
                dve.wait_ge(S_y, u + 1)
                ve.bn_stats(stats[:, u % 2, :], xres[:, tile_of(u), :]).then_inc(S_st, 1)

            def mean_var(u):
                dve.wait_ge(S_st, u + 1)
                if u >= 2 * G:
                    dve.wait_ge(S_x1, u - 2 * G + 1)
                ve.bn_aggr(mv[:, u // G % 2, u % G, :], stats[:, u % 2, :]).then_inc(S_mv, 1)

            def variances(g):
                dve.wait_ge(S_mv, (g + 1) * G)
                ts(vv[:, :, 0], mv[:, g % 2, :, 1], LN_EPS, None, ALU.add)
                ts(vv[:, :, 1], mv[:, g % 2, :, 1], 1.0 + RMS_EPS, RMS_EPS * LN_EPS, ALU.mult, ALU.add).then_inc(S_vv, 1)

            def newton1(g):
                dve.wait_ge(S_rs, g + 1)
                tt(rsq[:], r0[:], r0[:], ALU.mult).then_inc(S_n1, 1)

            def newton2(g):
                dve.wait_ge(S_n1, g + 1)
                stt(rh[:], rsq[:], -0.5, vv[:], ALU.mult, ALU.mult).then_inc(S_n2, 1)

            def newton3(g):
                dve.wait_ge(S_n2, g + 1)
                if g >= 2:
                    dve.wait_ge(S_x1, (g - 1) * G)
                stt(rstd[:, g % 2], rh[:], 1.5, r0[:], ALU.add, ALU.mult).then_inc(S_n3, 1)

            def normed(g, t):
                if t == 0:
                    dve.wait_ge(S_n3, g + 1)
                    if g >= 2:
                        dve.wait_ge(S_scat[g % 2], g // 2 * (G * 2 * 16))
                        dve.wait_ge(S_xnt, g - 1)
                y = xres[:, tile_of(g * G + t), :]
                ts(rows[:, g % 2, t, :, 0:D], y.unsqueeze(1).broadcast_to([P, 2, D]),
                   mv[:, g % 2, t, 0:1], rstd[:, g % 2, t, 1:2], ALU.subtract, ALU.mult).then_inc(S_xn, 1)

            def rank_experts(g):
                dve.wait_ge(S_rts, g + 1)
                for t in range(G):
                    last = ve.max(r8[:, t, :], sc[:, t, :])
                last.then_inc(S_r8, 1)

            def name_experts(g):
                dve.wait_ge(S_r8, g + 1)
                tt(sdif[:], r8[:, :, 1], r8[:, :, 0], ALU.subtract).then_inc(S_sd, 1)
                for t in range(G):
                    last = ve.max_index(ri[:, t, :], r8[:, t, :], sc[:, t, :])
                last.then_inc(S_ri, 1)

            def float_names(g):
                dve.wait_ge(S_ri, g + 1)
                ve.tensor_copy(idxf[:], ri[:, :, 0:2]).then_inc(S_id, 1)

            def onehots(g):
                dve.wait_ge(S_id, g + 1)
                for k in range(2):
                    last = tt(oh[:, k], iota8[:].unsqueeze(1).broadcast_to([P, G, EXPERTS]),
                              idxf[:, :, k:k + 1].broadcast_to([P, G, EXPERTS]), ALU.is_equal)
                last.then_inc(S_oh, 1)

            def choices(g):
                dve.wait_ge(S_oh, g + 1)
                tt(chosen[:], oh[:, 0], oh[:, 1], ALU.add).then_inc(S_ch, 1)

            def weight_den(g):
                dve.wait_ge(S_ed, g + 1)
                ts(eden[:], edif[:], 1.0, None, ALU.add).then_inc(S_en, 1)

            def weight0(g):
                dve.wait_ge(S_en, g + 1)
                ve.reciprocal(rows[:, g % 2, :, 0, D + 1], eden[:]).then_inc(S_w0, 1)

            def weight1(g):
                dve.wait_ge(S_w0, g + 1)
                tt(rows[:, g % 2, :, 1, D + 1], edif[:], rows[:, g % 2, :, 0, D + 1], ALU.mult).then_inc(S_w1, 1)

            def count_group(g):
                ve.tensor_reduce(cred[:], chosen[:].rearrange("p t e -> p e t"), X, ALU.add).then_inc(S_cr, 1)

            def add_count(g):
                dve.wait_ge(S_cr, g + 1)
                tt(count[:], count[:], cred[:], ALU.add).then_inc(S_ct, 1)

            def round_count(g):
                dve.wait_ge(S_ct, g + 1)
                dve.wait_ge(S_rk, g + 1)
                ve.tensor_copy(countb[:], count[:]).then_inc(S_cb, 1)

            def choose_rank(g):
                dve.wait_ge(S_rks, g + 1)
                tt(rko[:], oh[:], rk[:].rearrange("p (t e) -> p t e", e=EXPERTS).unsqueeze(1).broadcast_to([P, 2, G, EXPERTS]),
                   ALU.mult).then_inc(S_ro, 1)

            def position(g):
                dve.wait_ge(S_ro, g + 1)
                ve.tensor_reduce(posf[:], rko[:], X, ALU.add).then_inc(S_pf, 1)

            def int_position(g):
                dve.wait_ge(S_pf, g + 1)
                ve.tensor_copy(posi[:, g % 2], posf[:]).then_inc(S_pi, 1)

            top8(0)
            take8(0)
            for u in range(STEPS):
                if u + 1 < TILES:
                    top8(u + 1)
                if 2 <= u < TILES + 2:
                    tile_stats(u - 2)
                if u < TILES:
                    recip_sum(u)
                if (g := group(u, 6)) is not None:
                    newton1(g)
                if (g := group(u, 7)) is not None:
                    normed(g, 0)
                    normed(g, 1)
                if (g := group(u, 9)) is not None:
                    rank_experts(g)
                if (g := group(u, 10)) is not None:
                    onehots(g)
                if (g := group(u, 11)) is not None:
                    weight0(g)
                    count_group(g)
                if (g := group(u, 12)) is not None:
                    choose_rank(g)
                if u + 1 < TILES:
                    take8(u + 1)
                if 2 <= u < TILES + 2:
                    mean_var(u - 2)
                if (g := group(u, 6)) is not None:
                    newton2(g)
                if (g := group(u, 7)) is not None:
                    normed(g, 2)
                    normed(g, 3)
                if (g := group(u, 9)) is not None:
                    name_experts(g)
                if (g := group(u, 10)) is not None:
                    choices(g)
                if (g := group(u, 11)) is not None:
                    weight1(g)
                    add_count(g)
                if (g := group(u, 12)) is not None:
                    position(g)
                if u < TILES:
                    probs(u)
                if 1 <= u < TILES + 1:
                    residual(u - 1)
                if (g := group(u, 5)) is not None:
                    variances(g)
                if (g := group(u, 6)) is not None:
                    newton3(g)
                if (g := group(u, 9)) is not None:
                    float_names(g)
                if (g := group(u, 10)) is not None:
                    weight_den(g)
                if (g := group(u, 11)) is not None:
                    round_count(g)
                if (g := group(u, 12)) is not None:
                    int_position(g)

            def step(k, ins):
                ins.then_inc(S_tab, 1)
                dve.wait_ge(S_tab, k)

            dve.wait_ge(S_tots, 1)
            step(1, ts(ntf[:], total[0:1, :], float(P - 1), None, ALU.add))
            step(2, ve.tensor_copy(nti[:], ntf[:]))
            step(3, ve.tensor_copy(totali[:], total[0:1, :]))
            step(4, ts(nti[:], nti[:], 7, None, ALU.arith_shift_right))
            step(5, ve.tensor_copy(ntf[:], nti[:]))
            step(6, ve.tensor_tensor_scan(ends[:], ntf[:], zero8[:], 0.0, ALU.add, ALU.add))
            step(7, tt(past[:], tiota[:].unsqueeze(2).broadcast_to([1, FTILES, EXPERTS]),
                       ends[:].unsqueeze(1).broadcast_to([1, FTILES, EXPERTS]), ALU.is_ge))
            step(8, ts(step8[:], ntf[:], -float(P), float(CAP), ALU.mult, ALU.add))
            step(9, ve.tensor_reduce(tef[:], past[:, :, 0:EXPERTS - 1], X, ALU.add))
            step(10, tt(pstep[:], past[:], step8[:].unsqueeze(1).broadcast_to([1, FTILES, EXPERTS]), ALU.mult))
            step(11, ve.tensor_reduce(rowf[:], pstep[:, :, 0:EXPERTS - 1], X, ALU.add))
            step(12, stt(rowg[:], tiota[:], float(P), rowf[:], ALU.mult, ALU.add))
            step(13, ts(rowlim[:], total[0:1, EXPERTS - 1:EXPERTS], float((EXPERTS - 1) * CAP), None, ALU.add))
            step(14, ts(rowi[:], rowg[:], rowlim[:], None, ALU.min))
            step(15, ve.tensor_copy(te[:], tef[:]))
            ve.tensor_copy(zero8[:], ends[:]).then_inc(S_tabd, 1)

            def hidden(j, r):
                dve.wait_ge(S_si, j + 1)
                dve.wait_ge(S_uu, j + 1)
                tt(hh[:, r % 2, :], PS[:, 2, 0:HIDDEN], sg[:, r % 2, :], ALU.mult).then_inc(S_h, 1)

            def weighted(j, r, turn):
                dve.wait_ge(S_dn, j + 1)
                dve.wait_ge(S_ys[r], turn * 16)
                ts(yo[:, r, :], PS[:, 4, 0:D], xg[:, r, D + 1:ROW], None, ALU.mult).then_inc(S_yo, 1)

            hidden(0, 0)

            def tile(j, r, turn, more):
                if more:
                    hidden(j + 1, r + 1)
                weighted(j, r, turn)

            with dve.Fori(0, FTILES // RING) as it:
                for r in range(RING):
                    tile(it * RING + r, r, it, True)
            for j in range(FTILES // RING * RING, FTILES):
                tile(j, j % RING, j // RING, j + 1 < FTILES)

            def final_sum(g):
                c = yb[:, g * CH:(g + 1) * CH]
                dve.wait_ge(S_f1, g + 1)
                stt(c, xres[:, g * G:(g + 1) * G, :].rearrange("p t n -> p (t n)"), 2.0, ya[:, g * CH:(g + 1) * CH],
                    ALU.mult, ALU.add).then_inc(S_f2, 1)

            def final_stats(g):
                c = yb[:, g * CH:(g + 1) * CH]
                dve.wait_ge(S_f2, g + 1)
                for t in range(G):
                    last = ve.bn_stats(st2[:, g % 2, t, :], c[:, t * D:(t + 1) * D])
                last.then_inc(S_f3, 1)

            def final_mean(g):
                dve.wait_ge(S_f3, g + 1)
                for t in range(G):
                    last = ve.bn_aggr(mv2[:, g % 2, t, :], st2[:, g % 2, t, :])
                last.then_inc(S_f4, 1)

            def final_var(g):
                dve.wait_ge(S_f4, g + 1)
                ts(vv2[:, g % 2, :], mv2[:, g % 2, :, 1], LN_EPS, None, ALU.add).then_inc(S_l2, 1)

            def final_newton1(g):
                dve.wait_ge(S_f6, g + 1)
                tt(rq2[:, g % 2, :], r02[:, g % 2, :], r02[:, g % 2, :], ALU.mult).then_inc(S_m1, 1)

            def final_newton2(g):
                dve.wait_ge(S_m1, g + 1)
                stt(rh2[:, g % 2, :], rq2[:, g % 2, :], -0.5, vv2[:, g % 2, :], ALU.mult, ALU.mult).then_inc(S_m2, 1)

            def final_newton3(g):
                dve.wait_ge(S_m2, g + 1)
                stt(rs2[:, g % 2, :], rh2[:, g % 2, :], 1.5, r02[:, g % 2, :], ALU.add, ALU.mult).then_inc(S_m3, 1)

            def final_norm(g):
                dve.wait_ge(S_m3, g + 1)
                for t in range(G):
                    at = slice((g * G + t) * D, (g * G + t + 1) * D)
                    last = ts(ya[:, at], yb[:, at], mv2[:, g % 2, t, 0:1], rs2[:, g % 2, t:t + 1], ALU.subtract, ALU.mult)
                last.then_inc(S_f7, 1)

            for g in range(NG + 1):
                if g < NG:
                    final_sum(g)
                if g >= 1:
                    final_newton1(g - 1)
                if g < NG:
                    final_stats(g)
                if g >= 1:
                    final_newton2(g - 1)
                if g < NG:
                    final_mean(g)
                if g >= 1:
                    final_newton3(g - 1)
                if g < NG:
                    final_var(g)
                if g >= 1:
                    final_norm(g - 1)

        @block.gpsimd
        def _(pool):
            gp = nc.gpsimd
            gp.dma_start(xres[:], io["mu"].rearrange("(t p) n -> p t n", p=P)).then_inc(S_x, 16)

            def add_bias(b):
                v = xres[:, b * BT:(b + 1) * BT, :]
                gp.tensor_tensor(v, v, bias_bc[:].unsqueeze(1).broadcast_to([P, BT, D]), ALU.add).then_inc(S_xb, 1)

            def sum_window(c, h, projected):
                pool.wait_ge(S_sil, c + 1)
                gp.tensor_tensor(sum2[:], sil[:, 0:2, :], sil[:, 2:4, :], ALU.add).then_inc(S_s2, 1)
                pool.wait_ge(S_s2, c + 1)
                pool.wait_ge(S_l, projected)
                gp.tensor_tensor(locT[:, h, :], sum2[:, 0, :], sum2[:, 1, :], ALU.add).then_inc(S_loc, 1)

            pool.wait_ge(S_x, 16)
            pool.wait_ge(S_foldc, 3)
            for b in range(B):
                add_bias(b)
            sum_window(0, 0, 0)
            with pool.Fori(0, B - 1) as b:
                sum_window(b * 2 + 1, 1, b * 2)
                sum_window(b * 2 + 2, 0, b * 2 + 1)
            sum_window(CHUNKS - 1, 1, CHUNKS - 2)
            pool.wait_ge(S_f, 32)
            pool.wait_ge(S_w, 16 * WLOADS)
            pool.wait_ge(S_c, 16 * CLOADS)
            gp.tensor_scalar(wr[:], wr[:], cols[:, 3:4], 1.0, ALU.mult, ALU.mult).then_inc(S_wrs, 1)
            gp.tensor_scalar(wup[:], wup[:], cols[:, 3:4], 1.0, ALU.mult, ALU.mult).then_inc(S_wsc, 1)

            pool.wait_ge(S_c, 16 * CLOADS)
            for u in range(STEPS):
                if (g := group(u, 7)) is not None:
                    pool.wait_ge(S_xn, (g + 1) * G)
                    pool.wait_ge(S_n3, g + 1)
                    for t in range(G):
                        seq, i = ORDER[g * G + t]
                        y = xres[:, seq * BT + i, :]
                        gp.tensor_scalar(y, y, mv[:, g % 2, t, 0:1], rstd[:, g % 2, t, 0:1], ALU.subtract, ALU.mult).then_inc(S_x1, 1)
                if (g := group(u, 12)) is not None:
                    if g >= 2:
                        pool.wait_ge(S_scat[g % 2], g // 2 * (G * 2 * 16))
                    gp.tensor_copy(rows[:, g % 2, :, :, D:D + 1].bitcast(I32).rearrange("p t k o -> p t (k o)"),
                                   dsts[:, g * G:(g + 1) * G, :]).then_inc(S_ds, 1)
                    pool.wait_ge(S_ds, g + 1)
                    pool.wait_ge(S_pi, g + 1)
                    pool.wait_ge(S_w1, g + 1)
                    for t in range(G):
                        for k in range(2):
                            gp.indirect_dma_start(
                                buckets, bass.IndirectOffsetOnAxis(ap=posi[:, g % 2, k, t:t + 1], axis=0),
                                rows[:, g % 2, t, k, :], None).then_inc(S_scat[g % 2], 16)

            def scatter(j, r):
                pool.wait_ge(S_yo, j + 1)
                settled(pool)
                gp.indirect_dma_start(
                    ydram, bass.IndirectOffsetOnAxis(ap=xg[:, r, D:D + 1].bitcast(I32), axis=0),
                    yo[:, r, :], None, bounds_check=PAIRS - 1, oob_is_err=False).then_inc(S_ys[r], 16)

            with pool.Fori(0, FTILES // RING) as it:
                for r in range(RING):
                    scatter(it * RING + r, r)
            for j in range(FTILES // RING * RING, FTILES):
                scatter(j, j % RING)
            for g in range(NG):
                pool.wait_ge(S_ya[g], 32)
                gp.tensor_tensor(ya[:, g * CH:(g + 1) * CH], ya[:, g * CH:(g + 1) * CH], yb[:, g * CH:(g + 1) * CH], ALU.add).then_inc(S_f1, 1)


def kernel(**inputs):
    import ml_dtypes
    import concourse.bacc as bacc
    from concourse.bass_utils import run_bass_kernel_spmd

    g = {k.replace("L0_attn_", "").replace("L0_ffn_", ""): np.asarray(v) for k, v in inputs.items()}
    c = np.ascontiguousarray
    mu = g["mu"].reshape(T, D)
    arrays = {
        "mu": c(mu), "muT": c(mu.T), "Wq": c(g["Wq"]), "Wk": c(g["Wk"]), "Wm1": c(g["Wm1"]), "Wo": c(g["Wo"]),
        "WvT": c(g["Wv"].T), "Wm2T": c(g["Wm2"].T),
        "cols": c(np.stack([g["bq"], g["bk"], g["bm1"], g["norm_scale"]], axis=1)),
        "reps": c(np.stack([np.broadcast_to(g["bm2"][:, None], (D, P)), np.broadcast_to(g["bv"][:, None], (D, P)),
                            np.broadcast_to(g["bo"][None, :], (P, D))], axis=1)),
        "wrT": c(g["w_router"].T),
        "wupT": c(g["w_up"].transpose(2, 0, 1).reshape(D, EXPERTS * 2 * HIDDEN)),
        "wdnT": c(g["w_down"].transpose(2, 0, 1).reshape(2, P, EXPERTS, D).transpose(1, 2, 0, 3).reshape(P, EXPERTS * HIDDEN)),
    }
    r = np.arange(P)
    arrays["ident"] = np.eye(P, dtype=np.float32)
    arrays["cbf"] = np.stack([np.eye(P), np.where(r[None, :] > r[:, None], MASKED, 0.0),
                              r[:, None] < r[None, :], np.ones((P, P))], axis=1).astype(ml_dtypes.bfloat16)
    arrays["ebase"] = np.broadcast_to(np.tile(np.arange(EXPERTS) * CAP, G), (P, G * EXPERTS)).astype(ml_dtypes.bfloat16)
    arrays["iota8"] = np.broadcast_to(np.arange(EXPERTS, dtype=np.float32), (P, EXPERTS)).copy()
    arrays["dsts"] = (r[:, None, None] + np.array([seq * BT + i for seq, i in ORDER])[None, :, None] * P + np.arange(2)[None, None, :] * T).astype(np.int32)
    arrays["tiota"] = np.arange(FTILES, dtype=np.float32)[None, :]
    arrays["epsc"] = np.broadcast_to(np.array([LN_EPS, RMS_EPS * LN_EPS], np.float32), (P, 2)).copy()

    nc = bacc.Bacc("TRN2", target_bir_lowering=False, num_devices=1)
    io = {k: nc.dram_tensor(f"in_{k}", a.shape, mybir.dt.from_np(a.dtype), kind="ExternalInput").ap() for k, a in arrays.items()}
    io["out"] = nc.dram_tensor("out", [T, D], mybir.dt.float32, kind="ExternalOutput").ap()
    build(nc, io)
    res = run_bass_kernel_spmd(nc, [{f"in_{k}": a for k, a in arrays.items()}], core_ids=[0])
    return res.results[0]["out"].reshape(B, N, D)
```

```python
import numpy as np
import concourse.bass as bass
from concourse import mybir
from contextlib import ExitStack

P = 128
B, N, D = 4, 1024, 128
T = B * N
TILES = T // P
BT = N // P
WINDOW = 4
TOPK = 8
EXPERTS, HIDDEN = 8, 256
CH = 512
CHUNKS = T // CH
CT = CH // P
G = 4
NG = TILES // G
LN_EPS, RMS_EPS = 1e-5, 1e-6
SCALE = float(1.0 / np.sqrt(D))
MASKED = -1e30
TAKEN = -3e38
CAP = T + P
ROW = D + 3
PAIRS = 2 * T
FTILES = PAIRS // P + EXPERTS - 1
RING = 16
OCTET = 8
DIGITS = 6
AHEAD = 2
WORDS = -(-(RING + AHEAD) // DIGITS)
EARLY = 6
FIRST = 2 * RING
assert FIRST <= EARLY * G * 2 - EXPERTS + 1
WHOLE = FTILES // RING * RING
TURNS = -(-FTILES // RING)
LOOKED = (TURNS - 1) * RING + WORDS * DIGITS
TABLE = (TURNS + 1) * RING
SLOTS = 4
NOWHERE = 1 << 20


ORDER = [(s, i) for s in range(B) for i in (range(BT) if s % 2 == 0 else range(BT - 1, -1, -1))]


def build(nc, io):
    F32, BF16 = mybir.dt.float32, mybir.dt.bfloat16
    I32, U32 = mybir.dt.int32, mybir.dt.uint32
    ALU = mybir.AluOpType
    ACT = mybir.ActivationFunctionType
    X = mybir.AxisListType.X

    ctx = ExitStack()
    with ctx:
        def sb(name, shape, dt=F32):
            return ctx.enter_context(nc.sbuf_tensor(name, shape, dt))

        def sem(name):
            return ctx.enter_context(nc.semaphore(name))

        buckets = nc.dram_tensor("buckets", [EXPERTS * CAP, ROW], F32, kind="Internal").ap()
        ydram = nc.dram_tensor("expert_out", [PAIRS, D], F32, kind="Internal").ap()

        wq = sb("wq", [P, D]); wk = sb("wk", [P, D])
        wm1 = sb("wm1", [P, 2, D])
        wo = sb("wo", [P, 2, D])
        wvT = sb("wvT", [P, D]); wm2T = sb("wm2T", [P, D])
        cols = sb("cols", [P, 4])
        reps = sb("reps", [P, 3, P])
        ident = sb("ident", [P, P])
        cbf = sb("cbf", [P, 4, P], BF16)
        ebase = sb("ebase", [P, G * EXPERTS], BF16)
        iota8 = sb("iota8", [P, EXPERTS])
        dsts = sb("dsts", [P, TILES, 2], I32)
        tiota = sb("tiota", [1, TABLE])
        pow8 = sb("pow8", [1, DIGITS])
        epsc = sb("epsc", [P, 2])
        wvo = sb("wvo", [P, D]); w2o = sb("w2o", [P, D]); bias_bc = sb("bias_bc", [P, D])
        wr = sb("wr", [P, EXPERTS])
        wup = sb("wup", [P, EXPERTS * 2 * HIDDEN])
        wdn = sb("wdn", [P, EXPERTS * HIDDEN])

        xres = sb("xres", [P, TILES, D])
        qT = sb("qT", [P, T]); kT = sb("kT", [P, T]); vp = sb("vp", [P, TILES * D])

        spare = sb("spare", [P, EXPERTS * 2 * HIDDEN])
        xTc = sb("xTc", [P, 2, CH])
        cb = sb("cb", [P, WINDOW + N])
        pre = spare[:, 0:WINDOW * CH].rearrange("p (w n) -> p w n", n=CH); sil = sb("sil", [P, WINDOW, CH])
        sum2 = spare[:, WINDOW * CH:(WINDOW + 2) * CH].rearrange("p (w n) -> p w n", n=CH)
        locT = spare[:, (WINDOW + 2) * CH:(WINDOW + 4) * CH].rearrange("p (w n) -> p w n", n=CH)
        F32R = mybir.dt.float32r
        wuph = spare[:].bitcast(F32R); wupl = wup[:].bitcast(F32R)

        ex = sb("ex", [P, 3, N])
        pr = sb("pr", [P, 3, N])
        top = sb("top", [P, 2, 8]); nbias = sb("nbias", [P, 2]); e8 = sb("e8", [P, 2, 8])
        lsum = sb("lsum", [P, 2]); rl = sb("rl", [P, 4])
        pT = sb("pT", [P, 4, CH])
        stats = sb("stats", [P, 2, 6])
        mv = sb("mv", [P, SLOTS, G, 2]); vv = sb("vv", [P, G, 2]); lnv = sb("lnv", [P, G, 2])
        r0 = sb("r0", [P, G, 2]); rsq = sb("rsq", [P, G, 2]); rh = sb("rh", [P, G, 2])
        rstd = sb("rstd", [P, G, 2]); rrs = sb("rrs", [P, G])
        rstd2 = sb("rstd2", [P, SLOTS, G]); nmr = sb("nmr", [P, SLOTS, G])
        xnT = sb("xnT", [P, G * P])
        rows = sb("rows", [P, SLOTS, G, 2, ROW])
        sc = sb("sc", [P, G, EXPERTS])
        r8 = sb("r8", [P, G, 8]); ri = sb("ri", [P, G, 8], U32)
        idxf = sb("idxf", [P, G, 2]); oh = sb("oh", [P, 2, G, EXPERTS])
        chosen = sb("chosen", [P, G, EXPERTS], BF16)
        count = sb("count", [P, EXPERTS]); countb = sb("countb", [P, EXPERTS], BF16)
        cred = sb("cred", [P, EXPERTS])
        sdif = sb("sdif", [P, G]); edif = sb("edif", [P, G]); eden = sb("eden", [P, G])
        rk = sb("rk", [P, G * EXPERTS]); rko = sb("rko", [P, 2, G, EXPERTS])
        posf = sb("posf", [P, 2, G]); posi = sb("posi", [P, SLOTS, 2, G], I32)
        total = sb("total", [P, EXPERTS]); ntf = sb("ntf", [1, EXPERTS])
        totali = sb("totali", [1, EXPERTS], I32); nti = sb("nti", [1, EXPERTS], I32)
        zero8 = sb("zero8", [1, EXPERTS]); sums = sb("sums", [1, EXPERTS]); taken = sb("taken", [1, EXPERTS])
        left = sb("left", [1, EXPERTS]); start0 = sb("start0", [1, 1]); ends = sb("ends", [1, EXPERTS])
        past = sb("past", [1, TABLE, EXPERTS]); step8 = sb("step8", [1, EXPERTS])
        pstep = sb("pstep", [1, TABLE, EXPERTS])
        tef = sb("tef", [1, TABLE]); rowf = sb("rowf", [1, TABLE]); rowg = sb("rowg", [1, TABLE])
        rowlim = sb("rowlim", [1, 1])
        tew = sb("tew", [1, TURNS, WORDS, DIGITS]); packf = sb("packf", [1, TURNS, WORDS])
        pack = sb("pack", [1, TURNS, WORDS], I32)
        rowi = sb("rowi", [1, TABLE], I32)
        pad = sb("pad", [P, ROW])
        xg = sb("xg", [P, RING, ROW]); xgh = sb("xgh", [P, 2, P], F32R); xgl = sb("xgl", [P, 2, P], F32R)
        sg = sb("sg", [P, 2, HIDDEN]); hh = sb("hh", [P, 2, HIDDEN]); hT = sb("hT", [P, 2, HIDDEN])
        skip = cb[:, 0:2 * D].rearrange("p (s n) -> p s n", n=D)
        yo = sil[:].rearrange("p w n -> p (w n)").rearrange("p (r n) -> p r n", n=D)
        ya = qT; yb = kT
        st2 = sb("st2", [P, 2, G, 6]); mv2 = sb("mv2", [P, 2, G, 2])
        vv2 = sb("vv2", [P, 2, G]); ln2 = sb("ln2", [P, 2, G]); r02 = sb("r02", [P, 2, G])
        rq2 = sb("rq2", [P, 2, G]); rh2 = sb("rh2", [P, 2, G]); rs2 = sb("rs2", [P, 2, G]); nm2 = sb("nm2", [P, 2, G])

        PS = ctx.enter_context(nc.psum_tensor("PS", [P, 8, 512], F32))
        def score(slot, w):
            return PS[:, 2 * slot:2 * slot + 2, :].rearrange("p a n -> p (a n)")[:, 0:w]

        S_w = sem("weights_loaded"); S_p = sem("projection_weights_loaded"); S_c = sem("constants_loaded"); S_f = sem("ffn_weights_loaded")
        S_x = sem("x_loaded")
        S_xT = [sem("xT_loaded0"), sem("xT_loaded1")]
        S_init = sem("pads_set"); S_fold = sem("weights_folded"); S_foldc = sem("folded_copied")
        S_q = sem("q_made"); S_k = sem("k_made"); S_a = sem("a_made"); S_cc = sem("c_made"); S_v = sem("v_made")
        S_qs = sem("q_stored"); S_ks = sem("k_stored"); S_cs = sem("c_stored"); S_vs = sem("v_stored")
        S_pre = sem("preact_made"); S_sil = sem("silu_made"); S_s2 = sem("silu_pairs_summed")
        S_loc = sem("local_summed"); S_l = sem("local_projected");
        S_base = sem("base_made")
        S_sc = sem("scores_made"); S_top = sem("top8_found"); S_nb = sem("neg_max_made")
        S_ex = sem("exp_made"); S_ls = sem("exp_sum_made"); S_mt = sem("top8_taken"); S_pr = sem("probs_made")
        S_tp = sem("probs_transposed"); S_ts = sem("probs_T_stored"); S_pv = sem("attention_out_made")

        S_rl = sem("recip_sum_made"); S_y = sem("y_made"); S_st = sem("stats_made"); S_mv = sem("mean_var_made")
        S_ln = sem("ln_var_made"); S_rs = sem("rstd_made"); S_xn = sem("xn_made")
        S_xnt = sem("xn_transposed"); S_xns = sem("xn_T_stored"); S_rt = sem("router_made"); S_rts = sem("router_stored")
        S_r8 = sem("router_sorted"); S_ri = sem("router_ranked"); S_id = sem("choice_float"); S_oh = sem("onehot_made")
        S_ch = sem("chosen_made"); S_cr = sem("chosen_counted"); S_ct = sem("count_updated"); S_cb = sem("count_copied")
        S_sd = sem("score_gap_made"); S_ed = sem("exp_gap_made"); S_en = sem("gap_den_made")
        S_w0 = sem("weight0_made"); S_w1 = sem("weight1_made")
        S_rk = sem("rank_made"); S_rks = sem("rank_stored"); S_ro = sem("rank_chosen"); S_pf = sem("position_made")
        S_pi = sem("position_int"); S_ds = sem("dst_written"); S_scat = [sem(f"scattered{i}") for i in range(SLOTS)]; S_nm = sem("scale_and_shift_made"); S_rr = sem("recip_rstd_made"); S_sk = sem("skip_share_made")
        S_tot = sem("totals_made"); S_tots = sem("totals_stored"); S_tab = sem("table_step"); S_taba = sem("first_tiles_tabled"); S_tabd = sem("tables_done")
        S_padv = sem("pad_made"); S_padw = sem("pad_written"); S_wsc = sem("up_scaled"); S_wrs = sem("router_scaled")
        S_g = [sem(f"rows_loaded{i}") for i in range(RING)]
        S_gt = sem("rows_transposed"); S_gs = sem("rows_T_stored"); S_gl = sem("rest_of_rows_T_stored"); S_uu = sem("up_made")
        S_si = sem("gate_silu_made"); S_h = sem("h_made"); S_ht = sem("h_transposed"); S_hs = sem("h_T_stored")
        S_dn = sem("down_made"); S_yo = sem("y_weighted"); S_ss = sem("skips_made")
        S_ys = [sem(f"y_scattered{i}") for i in range(RING)]
        S_ya = [sem(f"y_fetched{i}") for i in range(NG)]
        S_f1 = sem("choices_added"); S_f3 = sem("final_stats"); S_f4 = sem("final_mean_var")
        S_vv = sem("variance_biased"); S_n1 = sem("rstd_squared"); S_n2 = sem("rstd_error_made"); S_n3 = sem("rstd_refined")
        S_l2 = sem("final_vars"); S_m1 = sem("final_rstd_squared"); S_m2 = sem("final_rstd_error"); S_m3 = sem("final_rstd_refined"); S_m4 = sem("final_shift_made")
        S_f5 = sem("final_ln"); S_f6 = sem("final_rstd"); S_f7 = sem("final_normed"); S_f8 = sem("final_first_normed"); S_out = sem("out_stored"); S_passed = sem("waits_passed")

        block = ctx.enter_context(nc.Block())
        WLOADS, PLOADS, CLOADS = 6, 3, 8

        def group(u, back, slack=0):
            for late, groups in ((slack, range(NG - TIGHT)), (0, range(NG - TIGHT, NG - 1)), (-2, range(NG - 1, NG))):
                g, r = divmod(u - back - late, G)
                if r == 0 and g in groups:
                    return g
            return None

        def tile_of(u):
            return ORDER[u][0] * BT + ORDER[u][1]

        def settled(engine):
            engine.sem_inc(S_passed, 1)

        W = [(i + 1) * P for _, i in ORDER]
        LAX = 1
        TIGHT = 2
        TOTAL_STEP = EARLY * G + 9
        STEPS = TILES + 7
        QUADS = [-(-w // CH) for w in W]
        QUADS_BEFORE = [sum(QUADS[:u]) for u in range(TILES + 1)]
        ALLSCAT = NG // SLOTS * G * 2 * 16

        @block.sync
        def _(sp):
            sp.dma_start(wm1[:], io["Wm1"].rearrange("(a p) n -> p a n", p=P)).then_inc(S_p, 16)
            sp.dma_start(xTc[:, 0, :], io["muT"][:, 0:CH]).then_inc(S_xT[0], 16)
            for dst, src in ((wq[:], io["Wq"]), (wk[:], io["Wk"])):
                sp.dma_start(dst, src).then_inc(S_p, 16)
            sp.dma_start(xTc[:, 1, :], io["muT"][:, CH:2 * CH]).then_inc(S_xT[1], 16)
            with sp.Fori(1, B) as b:
                for h in range(2):
                    sp.wait_ge(S_v, b * 2 + (h - 1))
                    sp.dma_start(xTc[:, h, :], io["muT"][:, bass.ds(b * N + h * CH, CH)]).then_inc(S_xT[h], 16)
            sp.dma_start(wup[:], io["wupT"]).then_inc(S_f, 16)
            sp.dma_start(wdn[:], io["wdnT"]).then_inc(S_f, 16)

            def load_rows(j, n, slot, turn, first=False):
                row = nc.values_load_multi_w_load_instructions(
                    rowi[0:1, bass.ds(j, n)], engines=(mybir.EngineType.SP,), min_val=0, max_val=EXPERTS * CAP - P)[1]
                if first:
                    for i, done in enumerate(S_scat):
                        sp.wait_ge(done, len(range(i, EARLY, SLOTS)) * G * 2 * 16)
                for r in range(n):
                    if not (isinstance(turn, int) and turn == 0):
                        sp.wait_ge(S_ys[slot + r], turn * 16)
                    sp.dma_start(xg[:, slot + r, :], buckets[bass.ds(row[r], P), :]).then_inc(S_g[slot + r], 16)

            sp.wait_ge(S_taba, 1)
            load_rows(0, OCTET, 0, 0, True)
            load_rows(OCTET, OCTET, OCTET, 0)
            sp.wait_ge(S_padv, 1)
            sp.wait_ge(S_tabd, 1)
            cnt = nc.values_load_multi_w_load_instructions(totali[0:1, :], engines=(mybir.EngineType.SP,), min_val=0, max_val=T)[1]
            for e in range(EXPERTS):
                sp.dma_start(buckets[bass.ds(cnt[e] + e * CAP, P), :], pad[:]).then_inc(S_padw, 16)
            with sp.Fori(1, FIRST // RING) as it:
                load_rows(it * RING, OCTET, 0, it)
                load_rows(it * RING + OCTET, OCTET, OCTET, it)
            sp.wait_ge(S_padw, 16 * EXPERTS)
            for done in S_scat:
                sp.wait_ge(done, ALLSCAT)
            with sp.Fori(FIRST // RING, FTILES // RING) as it:
                load_rows(it * RING, OCTET, 0, it)
                load_rows(it * RING + OCTET, OCTET, OCTET, it)
            load_rows(WHOLE, FTILES - WHOLE, 0, WHOLE // RING)
            for r in range(RING):
                sp.wait_ge(S_ys[r], 16 * (-(-(FTILES - r) // RING)))
            y0 = ydram[0:T, :].rearrange("(g p t) n -> g p (t n)", t=G, p=P)
            y1 = ydram[T:2 * T, :].rearrange("(g p t) n -> g p (t n)", t=G, p=P)
            for g in range(NG):
                sp.dma_start(ya[:, g * CH:(g + 1) * CH], y0[g]).then_inc(S_ya[g], 16)
                sp.dma_start(yb[:, g * CH:(g + 1) * CH], y1[g]).then_inc(S_ya[g], 16)
            out = io["out"].rearrange("(g t p) n -> g p t n", t=G, p=P)
            for g in range(NG):
                sp.wait_ge(S_f7, g + 1)
                sp.wait_ge(S_f8, g // 2 + 1)
                sp.dma_start(out[g], yb[:, g * CH:(g + 1) * CH].rearrange("p (t n) -> p t n", n=D)).then_inc(S_out, 16)
            sp.wait_ge(S_out, 16 * NG)

        @block.tensor
        def _(pe):
            mm = nc.tensor.matmul

            def fold():
                pe.wait_ge(S_w, 16 * WLOADS)
                mm(PS[:, 6, 0:D], wvT[:], wo[:, 1, :], start=True, stop=True)
                mm(PS[:, 6, D:2 * D], wm2T[:], wo[:, 0, :], start=True, stop=True)
                mm(PS[:, 6, 2 * D:3 * D], reps[:, 0, :], wo[:, 0, :], start=True, stop=False)
                mm(PS[:, 6, 2 * D:3 * D], reps[:, 1, :], wo[:, 1, :], start=False, stop=False)
                mm(PS[:, 6, 2 * D:3 * D], ident[:], reps[:, 2, :], start=False, stop=True).then_inc(S_fold, 1)

            def project(c, h, b):
                pe.wait_ge(S_xT[h], b * 16 + 16)
                for bank, w, made, stored in ((3, wm1[:, 1, :], S_cc, S_cs), (2, wm1[:, 0, :], S_a, S_pre),
                                              (0, wq[:], S_q, S_qs), (1, wk[:], S_k, S_ks)):
                    if not (isinstance(c, int) and c == 0):
                        pe.wait_ge(stored, c)
                    mm(PS[:, bank, :], w, xTc[:, h, :], start=True, stop=True).then_inc(made, 1)
                if isinstance(c, int) and c == 0:
                    fold()
                    pe.wait_ge(S_foldc, 3)
                else:
                    pe.wait_ge(S_vs, c)
                for j in range(CT):
                    last = mm(PS[:, 4, j * D:(j + 1) * D], xTc[:, h, j * P:(j + 1) * P], wvo[:], start=True, stop=True)
                last.then_inc(S_v, 1)

            def local(c, h):
                pe.wait_ge(S_loc, c + 1)
                pe.wait_ge(S_base, c + 1)
                for j in range(CT):
                    last = mm(PS[:, 7, j * D:(j + 1) * D], locT[:, h, j * P:(j + 1) * P], w2o[:], start=True, stop=True)
                last.then_inc(S_l, 1)

            pe.wait_ge(S_p, 16 * PLOADS)
            project(0, 0, 0)
            project(1, 1, 0)
            with pe.Fori(0, B - 1) as b:
                project(b * 2 + 2, 0, b + 1)
                local(b * 2, 0)
                project(b * 2 + 3, 1, b + 1)
                local(b * 2 + 1, 1)
            pe.wait_ge(S_c, 16 * CLOADS)
            for s in (S_qs, S_ks, S_pre, S_cs, S_vs):
                pe.wait_ge(s, CHUNKS)

            def scores(u):
                (seq, i), w = ORDER[u], W[u]
                if u >= 2:
                    pe.wait_ge(S_ex, u - 1)
                for c0 in range(0, w, CH):
                    n = min(CH, w - c0)
                    mm(score(u % 2, w)[:, c0:c0 + n], qT[:, seq * N + i * P:seq * N + i * P + P],
                       kT[:, seq * N + c0:seq * N + c0 + n], start=True, stop=c0 + n < w)
                mm(score(u % 2, w)[:, i * P:w], cbf[:, 0, :], cbf[:, 1, :], start=False, stop=True).then_inc(S_sc, 1)

            def turn_probs(u):
                i, slot = ORDER[u][1], u % 3
                pe.wait_ge(S_pr, u + 1)
                for g in range(QUADS[u]):
                    q = QUADS_BEFORE[u] + g
                    if q >= 2:
                        pe.wait_ge(S_ts, q - 1)
                    for m in range(g * CT, min((g + 1) * CT, i + 1)):
                        last = nc.tensor.transpose(PS[:, 4 + q % 2, (m - g * CT) * P:(m - g * CT + 1) * P],
                                                   pr[:, slot, m * P:(m + 1) * P], ident[:])
                    last.then_inc(S_tp, 1)

            def attend(u):
                seq, i = ORDER[u]
                for g in range(QUADS[u]):
                    q = QUADS_BEFORE[u] + g
                    pe.wait_ge(S_ts, q + 1)
                    if g == 0 and u >= 1:
                        pe.wait_ge(S_y, u)
                    for m in range(g * CT, min((g + 1) * CT, i + 1)):
                        last = mm(PS[:, 6, 0:D], pT[:, q % 4, (m - g * CT) * P:(m - g * CT + 1) * P],
                                  vp[:, seq * N + m * D:seq * N + (m + 1) * D], start=m == 0, stop=m == i)
                    last.then_inc(S_pv, 1)

            def turn_xn(g):
                pe.wait_ge(S_xn, (g + 1) * G)
                if g == 0:
                    pe.wait_ge(S_base, CHUNKS + 1)
                else:
                    pe.wait_ge(S_rks, g)
                for t in range(G):
                    last = nc.tensor.transpose(PS[:, 7, t * P:(t + 1) * P], rows[:, g % SLOTS, t, 0, 0:D], ident[:])
                last.then_inc(S_xnt, 1)

            def route(g):
                if g == 0:
                    pe.wait_ge(S_wrs, 1)
                pe.wait_ge(S_xns, g + 1)
                for t in range(G):
                    last = mm(PS[:, 7, t * EXPERTS:(t + 1) * EXPERTS], xnT[:, t * P:(t + 1) * P], wr[:], start=True, stop=True)
                last.then_inc(S_rt, 1)

            def rank(g):
                pe.wait_ge(S_rts, g + 1)
                pe.wait_ge(S_ch, g + 1)
                if g == EARLY:
                    pe.wait_ge(S_tots, 1)
                if g >= 1:
                    pe.wait_ge(S_cb, g + 1)
                r = PS[:, 7, 0:G * EXPERTS]
                mm(r, cbf[:, 2, :], chosen[:].rearrange("p t e -> p (t e)"), start=True, stop=False)
                mm(r, cbf[:, 0, :], ebase[:], start=False, stop=False)
                for j in range(G - 1):
                    k = G - 1 - j
                    mm(r[:, (j + 1) * EXPERTS:], cbf[:, 3, :], chosen[:, j:j + 1, :].broadcast_to([P, k, EXPERTS]),
                       start=False, stop=False, skip_group_check=True)
                mm(r, cbf[:, 3, :], countb[:].unsqueeze(1).broadcast_to([P, G, EXPERTS]),
                   start=False, stop=True).then_inc(S_rk, 1)

            def totals(part):
                groups = (EARLY, NG)[part]
                pe.wait_ge(S_cb, groups + 1)
                if part == 0:
                    pe.wait_ge(S_rts, groups + 1)
                else:
                    pe.wait_ge(S_rks, groups)
                mm(PS[:, 7, 0:EXPERTS], cbf[:, 3, :], countb[:], start=True, stop=True).then_inc(S_tot, 1)

            pe.wait_ge(S_cb, 1)
            scores(0)
            scores(1)
            local(CHUNKS - 2, 0)
            for u in range(STEPS):
                if u == 1:
                    local(CHUNKS - 1, 1)
                if u + 2 < TILES:
                    scores(u + 2)
                if (g := group(u, 9)) is not None:
                    route(g)
                if u < TILES:
                    turn_probs(u)
                if 1 <= u < TILES + 1:
                    attend(u - 1)
                if u == TOTAL_STEP:
                    totals(0)
                if (g := group(u, 10, LAX)) is not None:
                    rank(g)
                if (g := group(u, 8)) is not None:
                    turn_xn(g)

            def experts(turn):
                return nc.values_load_multi_w_load_instructions(
                    pack[0:1, bass.ds(turn, 1), :].rearrange("p t w -> p (t w)"), engines=(mybir.EngineType.PE,),
                    min_val=0, max_val=EXPERTS ** DIGITS - 1)[1]

            def expert(words, r):
                return (words[r // DIGITS] >> (3 * (r % DIGITS))) & (EXPERTS - 1)

            pe.wait_ge(S_taba, 1)
            first = experts(0)
            totals(1)

            pe.wait_ge(S_f, 32)
            pe.wait_ge(S_wsc, 3)
            pe.wait_ge(S_tots, 2)

            def turn_rows(j, r, turn):
                pe.wait_ge(S_g[r % RING], turn * 16 + 16 * (r // RING) + 16)
                if not (isinstance(j, int) and j == 0):
                    pe.wait_ge(S_gl, j)
                nc.tensor.transpose(PS[:, 0, 0:P], xg[:, r % RING, 0:D], ident[:]).then_inc(S_gt, 1)

            def up(j, r, e):
                pe.wait_ge(S_gl, j + 1)
                if not (isinstance(j, int) and j < 2):
                    pe.wait_ge(S_h, j - 1)
                w = bass.ds(e * (2 * HIDDEN), 2 * HIDDEN)
                mm(PS[:, 1 + r % 2, :], xgl[:, r % 2, :], wuph[:, w], start=True, stop=False)
                mm(PS[:, 1 + r % 2, :], xgh[:, r % 2, :], wupl[:, w], start=False, stop=False)
                mm(PS[:, 1 + r % 2, :], xgh[:, r % 2, :], wuph[:, w], start=False, stop=True).then_inc(S_uu, 1)

            def turn_h(j, r):
                pe.wait_ge(S_h, j + 1)
                if not (isinstance(j, int) and j == 0):
                    pe.wait_ge(S_hs, j)
                for k in range(2):
                    last = nc.tensor.transpose(PS[:, 3, k * P:(k + 1) * P], hh[:, r % 2, k * P:(k + 1) * P], ident[:])
                last.then_inc(S_ht, 1)

            def down(j, r, e):
                pe.wait_ge(S_hs, j + 1)
                pe.wait_ge(S_yo, j + 1)
                for k in range(2):
                    last = mm(PS[:, 4, 0:D], hT[:, r % 2, k * P:(k + 1) * P],
                              wdn[:, bass.ds(e * HIDDEN + k * D, D)], start=k == 0, stop=k == 1)
                last.then_inc(S_dn, 1)

            turn_rows(0, 0, 0)
            turn_rows(1, 1, 0)
            up(0, 0, expert(first, 0))
            turn_rows(2, 2, 0)
            up(1, 1, expert(first, 1))
            turn_h(0, 0)

            def tile(j, r, turn, e, e2, left):
                if left > 3:
                    turn_rows(j + 3, r + 3, turn)
                if left > 2:
                    up(j + 2, r + 2, e2)
                if left > 1:
                    turn_h(j + 1, r + 1)
                down(j, r, e)

            def turn(it, words):
                for r in range(RING):
                    tile(it * RING + r, r, it, expert(words, r), expert(words, r + AHEAD), FTILES)

            turn(0, first)
            pe.wait_ge(S_tabd, 1)
            with pe.Fori(1, FTILES // RING) as it:
                turn(it, experts(it))
            words = experts(WHOLE // RING)
            for r in range(FTILES - WHOLE):
                tile(WHOLE + r, r, WHOLE // RING, expert(words, r), expert(words, r + AHEAD), FTILES - WHOLE - r)

        @block.scalar
        def _(act):
            ac = nc.scalar.activation
            for dst, src in ((cols[:], io["cols"]), (wvT[:], io["WvT"]), (wo[:], io["Wo"].rearrange("(a p) n -> p a n", p=P)),
                             (wm2T[:], io["Wm2T"]), (reps[:], io["reps"]), (ident[:], io["ident"])):
                act.dma_start(dst, src).then_inc(S_w, 16)
            for dst, src in ((cbf[:], io["cbf"]), (ebase[:], io["ebase"]), (iota8[:], io["iota8"]),
                             (dsts[:], io["dsts"]), (tiota[:], io["tiota"]), (epsc[:], io["epsc"]),
                             (wr[:], io["wrT"]), (pow8[:], io["pow8"])):
                act.dma_start(dst, src).then_inc(S_c, 16)
            act.wait_ge(S_w, 16 * WLOADS)
            ac(cb[:, 0:WINDOW], ident[:, 0:WINDOW], ACT.Identity, bias=cols[:, 2:3], scale=0.0).then_inc(S_init, 1)

            def store_folded():
                act.wait_ge(S_fold, 1)
                ac(wvo[:], PS[:, 6, 0:D], ACT.Copy).then_inc(S_foldc, 1)
                ac(w2o[:], PS[:, 6, D:2 * D], ACT.Copy, scale=1.0 / WINDOW).then_inc(S_foldc, 1)
                ac(bias_bc[:], PS[:, 6, 2 * D:3 * D], ACT.Copy).then_inc(S_foldc, 1)

            nc.scalar.preload_act_table(ACT.Silu)

            def store_projected(b, h, first=False):
                c = b * 2 + h
                act.wait_ge(S_cc, c + 1)
                if not first:
                    act.wait_ge(S_pre, c)
                ac(cb[:, WINDOW + h * CH:WINDOW + (h + 1) * CH], PS[:, 3, :], ACT.Identity,
                   bias=cols[:, 2:3]).then_inc(S_cs, 1)
                if first:
                    store_folded()
                act.wait_ge(S_q, c + 1)
                ac(qT[:, bass.ds(b * N + h * CH, CH)], PS[:, 0, :], ACT.Identity, bias=cols[:, 0:1]).then_inc(S_qs, 1)
                act.wait_ge(S_k, c + 1)
                ac(kT[:, bass.ds(b * N + h * CH, CH)], PS[:, 1, :], ACT.Identity, bias=cols[:, 1:2]).then_inc(S_ks, 1)
                act.wait_ge(S_pre, c + 1)
                if not first:
                    act.wait_ge(S_s2, c)
                ac(sil[:], pre, ACT.Silu).then_inc(S_sil, 1)

            store_projected(0, 0, True)
            store_projected(0, 1)
            with act.Fori(1, B) as b:
                for h in range(2):
                    store_projected(b, h)

            nc.scalar.preload_act_table_set("natural_log_exp_and_others")
            act.wait_ge(S_c, 16 * CLOADS)
            def exps(u):
                w, slot = W[u], u % 2
                act.wait_ge(S_nb, u + 1)
                if u >= 3:
                    act.wait_ge(S_pr, u - 2)
                ac(ex[:, u % 3, 0:w], score(slot, w), ACT.Exp, bias=nbias[:, slot:slot + 1], scale=SCALE).then_inc(S_ex, 1)
                if u >= 2:
                    act.wait_ge(S_rl, u - 1)
                ac(e8[:, slot, :], top[:, slot, :], ACT.Exp, bias=nbias[:, slot:slot + 1], scale=SCALE,
                   accum_out=lsum[:, slot:slot + 1]).then_inc(S_ls, 1)

            def store_probs(u):
                for g in range(QUADS[u]):
                    q = QUADS_BEFORE[u] + g
                    n = min(CH, W[u] - g * CH)
                    act.wait_ge(S_tp, q + 1)
                    if q >= 4:
                        act.wait_ge(S_pv, q - 3)
                    ac(pT[:, q % 4, 0:n], PS[:, 4 + q % 2, 0:n], ACT.Copy).then_inc(S_ts, 1)

            def first_rstd(g):
                act.wait_ge(S_vv, g + 1)
                ac(lnv[:], vv[:], ACT.Ln).then_inc(S_ln, 1)
                act.wait_ge(S_ln, g + 1)
                ac(r0[:], lnv[:], ACT.Exp, scale=-0.5).then_inc(S_rs, 1)

            def normed(g, tiles):
                act.wait_ge(S_nm, g + 1)
                if g >= SLOTS:
                    act.wait_ge(S_scat[g % SLOTS], g // SLOTS * (G * 2 * 16))
                    act.wait_ge(S_xnt, g - SLOTS + 1)
                for t in tiles:
                    y = xres[:, tile_of(g * G + t), :]
                    ac(rows[:, g % SLOTS, t, :, 0:D], y.unsqueeze(1).broadcast_to([P, 2, D]), ACT.Identity,
                       bias=nmr[:, g % SLOTS, t:t + 1], scale=rstd2[:, g % SLOTS, t:t + 1]).then_inc(S_xn, 1)

            def store_xn(g):
                act.wait_ge(S_xnt, g + 1)
                ac(xnT[:], PS[:, 7, :], ACT.Copy).then_inc(S_xns, 1)

            def store_route(g):
                act.wait_ge(S_rt, g + 1)
                if g >= 1:
                    act.wait_ge(S_ri, g)
                ac(sc[:], PS[:, 7, 0:G * EXPERTS].rearrange("p (t e) -> p t e", e=EXPERTS), ACT.Copy).then_inc(S_rts, 1)

            def gap(g):
                act.wait_ge(S_sd, g + 1)
                if g >= 1:
                    act.wait_ge(S_w1, g)
                ac(edif[:], sdif[:], ACT.Exp).then_inc(S_ed, 1)

            def store_rank(g):
                act.wait_ge(S_rk, g + 1)
                if g >= 1:
                    act.wait_ge(S_ro, g)
                ac(rk[:], PS[:, 7, 0:G * EXPERTS], ACT.Copy).then_inc(S_rks, 1)

            def store_totals(part):
                act.wait_ge(S_tot, part + 1)
                if part == 1:
                    act.wait_ge(S_taba, 1)
                ac(total[:], PS[:, 7, 0:EXPERTS], ACT.Copy).then_inc(S_tots, 1)

            exps(0)
            for u in range(STEPS):
                if (g := group(u, 9)) is not None:
                    store_xn(g)
                if u + 1 < TILES:
                    exps(u + 1)
                if (g := group(u, 8)) is not None and g < NG - 1:
                    normed(g, range(G // 2, G))
                if group(u, 7) == NG - 1:
                    normed(NG - 1, range(G))
                if (g := group(u, 9)) is not None:
                    store_route(g)
                if (g := group(u, 10, LAX)) is not None:
                    gap(g)
                    if g == NG - 1:
                        nc.scalar.preload_act_table(ACT.Silu)
                if u < TILES:
                    store_probs(u)
                if (g := group(u, 6)) is not None:
                    first_rstd(g)
                if (g := group(u, 7)) is not None and g < NG - 1:
                    normed(g, range(G // 2))
                if u == TOTAL_STEP:
                    store_totals(0)
                if (g := group(u, 10, LAX)) is not None:
                    store_rank(g)

            store_totals(1)

            def store_rows(j, r):
                act.wait_ge(S_gt, j + 1)
                ac(xgh[:, r % 2, :], PS[:, 0, 0:P], ACT.Copy).then_inc(S_gs, 1)

            def silu(j, r):
                act.wait_ge(S_uu, j + 1)
                ac(sg[:, r % 2, :], PS[:, 1 + r % 2, HIDDEN:2 * HIDDEN], ACT.Silu).then_inc(S_si, 1)

            def store_h(j, r):
                act.wait_ge(S_ht, j + 1)
                ac(hT[:, r % 2, :], PS[:, 3, 0:HIDDEN], ACT.Copy).then_inc(S_hs, 1)

            store_rows(0, 0)
            store_rows(1, 1)
            silu(0, 0)
            act.wait_ge(S_uu, 1)
            store_rows(2, 2)
            silu(1, 1)
            store_h(0, 0)

            def tile(j, r, left):
                if left > 3:
                    act.wait_ge(S_uu, j + 2)
                    store_rows(j + 3, r + 3)
                if left > 2:
                    silu(j + 2, r + 2)
                if left > 1:
                    store_h(j + 1, r + 1)

            with act.Fori(0, FTILES // RING) as it:
                for r in range(RING):
                    tile(it * RING + r, r, FTILES)
            for j in range(WHOLE, FTILES):
                tile(j, j % RING, FTILES - j)
            nc.scalar.preload_act_table_set("natural_log_exp_and_others")
            def final_norm(g):
                act.wait_ge(S_m4, g + 1)
                for t in range(1 - g % 2, G):
                    at = slice((g * G + t) * D, (g * G + t + 1) * D)
                    last = ac(yb[:, at], ya[:, at], ACT.Identity, bias=nm2[:, g % 2, t:t + 1], scale=rs2[:, g % 2, t:t + 1])
                last.then_inc(S_f7, 1)

            for g in range(NG):
                act.wait_ge(S_l2, g + 1)
                ac(ln2[:, g % 2, :], vv2[:, g % 2, :], ACT.Ln).then_inc(S_f5, 1)
                act.wait_ge(S_f5, g + 1)
                ac(r02[:, g % 2, :], ln2[:, g % 2, :], ACT.Exp, scale=-0.5).then_inc(S_f6, 1)
                if g >= 1:
                    final_norm(g - 1)
            final_norm(NG - 1)

        @block.vector
        def _(dve):
            ve = nc.vector
            ts, tt, stt = ve.tensor_scalar, ve.tensor_tensor, ve.scalar_tensor_tensor
            ve.memset(count[:], 0.0)
            ve.memset(zero8[:], 0.0)
            ve.memset(pad[:, 0:D], 0.0)
            ve.memset(pad[:, D:D + 1].bitcast(I32), NOWHERE)
            ve.memset(rows[:, :, :, 1, D + 2], 0.0)
            ve.memset(pad[:, D + 1:ROW], 0.0).then_inc(S_padv, 1)
            ve.memset(countb[:], 0.0).then_inc(S_cb, 1)
            dve.sem_inc(S_base, 1)
            dve.wait_ge(S_init, 1)

            def preact(c, h):
                dve.wait_ge(S_a, c + 1)
                dve.wait_ge(S_cs, c + 1)
                if not (isinstance(c, int) and c == 0):
                    dve.wait_ge(S_sil, c)
                a = PS[:, 2, :].unsqueeze(1).broadcast_to([P, WINDOW, CH])
                full = cb[:]
                near = bass.AP(tensor=full.tensor, offset=full.offset + h * CH,
                               ap=[full.ap[0], [1, WINDOW], [1, CH]])
                tt(pre, a, near, ALU.add).then_inc(S_pre, 1)

            def basis(c, b, h):
                dve.wait_ge(S_l, c + 1)
                v = xres[:, bass.ds(b * BT + h * CT, CT), :].rearrange("p t n -> p (t n)")
                tt(v, PS[:, 7, :], v, ALU.add).then_inc(S_base, 1)

            def store_v(c, b, h):
                dve.wait_ge(S_v, c + 1)
                tt(vp[:, bass.ds(b * N + h * CH, CH)].rearrange("p (t n) -> p t n", n=D), PS[:, 4, :].rearrange("p (t n) -> p t n", n=D),
                   bias_bc[:].unsqueeze(1).broadcast_to([P, CT, D]), ALU.add).then_inc(S_vs, 1)

            preact(0, 0)
            dve.wait_ge(S_foldc, 3)
            store_v(0, 0, 0)
            preact(1, 1)
            store_v(1, 0, 1)
            dve.wait_ge(S_x, 16)
            with dve.Fori(0, B - 1) as b:
                preact(b * 2 + 2, 0)
                store_v(b * 2 + 2, b + 1, 0)
                basis(b * 2, b, 0)
                preact(b * 2 + 3, 1)
                store_v(b * 2 + 3, b + 1, 1)
                basis(b * 2 + 1, b, 1)
            dve.wait_ge(S_c, 16 * CLOADS)
            def top8(u):
                s = u % 2
                dve.wait_ge(S_sc, u + 1)
                if u >= 2:
                    dve.wait_ge(S_ls, u - 1)
                ve.max(top[:, s, :], score(s, W[u])).then_inc(S_top, 1)

            def take8(u):
                s = u % 2
                dve.wait_ge(S_top, u + 1)
                if u >= 3:
                    dve.wait_ge(S_tp, QUADS_BEFORE[u - 2])
                ve.match_replace(pr[:, u % 3, 0:W[u]], top[:, s, :], score(s, W[u]), TAKEN).then_inc(S_mt, 1)
                ts(nbias[:, s:s + 1], top[:, s, 0:1], -SCALE, None, ALU.mult).then_inc(S_nb, 1)

            def probs(u):
                w, s = W[u], u % 3
                dve.wait_ge(S_mt, u + 1)
                dve.wait_ge(S_ex, u + 1)
                stt(pr[:, s, 0:w], pr[:, s, 0:w], TAKEN / 2, ex[:, s, 0:w], ALU.is_lt, ALU.mult).then_inc(S_pr, 1)

            def recip_sum(u):
                dve.wait_ge(S_ls, u + 1)
                if u >= 4:
                    dve.wait_ge(S_y, u - 3)
                ve.reciprocal(rl[:, u % 4:u % 4 + 1], lsum[:, u % 2:u % 2 + 1]).then_inc(S_rl, 1)

            def residual(u):
                dve.wait_ge(S_rl, u + 1)
                dve.wait_ge(S_pv, QUADS_BEFORE[u + 1])
                stt(xres[:, tile_of(u), :], PS[:, 6, 0:D], rl[:, u % 4:u % 4 + 1], xres[:, tile_of(u), :],
                    ALU.mult, ALU.add).then_inc(S_y, 1)

            def tile_stats(u):
                dve.wait_ge(S_y, u + 1)
                ve.bn_stats(stats[:, u % 2, :], xres[:, tile_of(u), :]).then_inc(S_st, 1)

            def mean_var(u):
                dve.wait_ge(S_st, u + 1)
                if u >= SLOTS * G:
                    dve.wait_ge(S_nm, u // G - SLOTS + 1)
                ve.bn_aggr(mv[:, u // G % SLOTS, u % G, :], stats[:, u % 2, :]).then_inc(S_mv, 1)

            def variances(g):
                dve.wait_ge(S_mv, (g + 1) * G)
                ts(vv[:, :, 0], mv[:, g % SLOTS, :, 1], LN_EPS, None, ALU.add)
                ts(vv[:, :, 1], mv[:, g % SLOTS, :, 1], 1.0 + RMS_EPS, RMS_EPS * LN_EPS, ALU.mult, ALU.add).then_inc(S_vv, 1)

            def newton1(g):
                dve.wait_ge(S_rs, g + 1)
                tt(rsq[:], r0[:], r0[:], ALU.mult).then_inc(S_n1, 1)

            def newton2(g):
                dve.wait_ge(S_n1, g + 1)
                stt(rh[:], rsq[:], -0.5, vv[:], ALU.mult, ALU.mult).then_inc(S_n2, 1)

            def newton3(g):
                dve.wait_ge(S_n2, g + 1)
                if g >= 1:
                    dve.wait_ge(S_sk, g)
                stt(rstd[:], rh[:], 1.5, r0[:], ALU.add, ALU.mult).then_inc(S_n3, 1)

            def scale_and_shift(g):
                dve.wait_ge(S_n3, g + 1)
                if g >= SLOTS:
                    dve.wait_ge(S_xn, (g - SLOTS + 1) * G)
                ve.tensor_copy(rstd2[:, g % SLOTS], rstd[:, :, 1])
                stt(nmr[:, g % SLOTS], mv[:, g % SLOTS, :, 0], -1.0, rstd[:, :, 1], ALU.mult, ALU.mult).then_inc(S_nm, 1)
                ve.reciprocal(rrs[:], rstd[:, :, 1]).then_inc(S_rr, 1)

            def skip_share(g):
                dve.wait_ge(S_rr, g + 1)
                if g >= SLOTS:
                    dve.wait_ge(S_scat[g % SLOTS], g // SLOTS * (G * 2 * 16))
                stt(rows[:, g % SLOTS, :, 0, D + 2], rstd[:, :, 0], 2.0, rrs[:], ALU.mult, ALU.mult).then_inc(S_sk, 1)

            def rank_experts(g):
                dve.wait_ge(S_rts, g + 1)
                for t in range(G):
                    last = ve.max(r8[:, t, :], sc[:, t, :])
                last.then_inc(S_r8, 1)

            def name_experts(g):
                dve.wait_ge(S_r8, g + 1)
                tt(sdif[:], r8[:, :, 1], r8[:, :, 0], ALU.subtract).then_inc(S_sd, 1)
                for t in range(G):
                    last = ve.max_index(ri[:, t, :], r8[:, t, :], sc[:, t, :])
                last.then_inc(S_ri, 1)

            def float_names(g):
                dve.wait_ge(S_ri, g + 1)
                ve.tensor_copy(idxf[:], ri[:, :, 0:2]).then_inc(S_id, 1)

            def onehots(g):
                dve.wait_ge(S_id, g + 1)
                for k in range(2):
                    last = tt(oh[:, k], iota8[:].unsqueeze(1).broadcast_to([P, G, EXPERTS]),
                              idxf[:, :, k:k + 1].broadcast_to([P, G, EXPERTS]), ALU.is_equal)
                last.then_inc(S_oh, 1)

            def choices(g):
                dve.wait_ge(S_oh, g + 1)
                tt(chosen[:], oh[:, 0], oh[:, 1], ALU.add).then_inc(S_ch, 1)

            def weight_den(g):
                dve.wait_ge(S_ed, g + 1)
                ts(eden[:], edif[:], 1.0, None, ALU.add).then_inc(S_en, 1)

            def weight0(g):
                dve.wait_ge(S_en, g + 1)
                ve.reciprocal(rows[:, g % SLOTS, :, 0, D + 1], eden[:]).then_inc(S_w0, 1)

            def weight1(g):
                dve.wait_ge(S_w0, g + 1)
                tt(rows[:, g % SLOTS, :, 1, D + 1], edif[:], rows[:, g % SLOTS, :, 0, D + 1], ALU.mult).then_inc(S_w1, 1)

            def count_group(g):
                ve.tensor_reduce(cred[:], chosen[:].rearrange("p t e -> p e t"), X, ALU.add).then_inc(S_cr, 1)

            def add_count(g):
                dve.wait_ge(S_cr, g + 1)
                tt(count[:], count[:], cred[:], ALU.add).then_inc(S_ct, 1)

            def round_count(g):
                dve.wait_ge(S_ct, g + 1)
                dve.wait_ge(S_rk, g + 1)
                ve.tensor_copy(countb[:], count[:]).then_inc(S_cb, 1)

            def choose_rank(g):
                dve.wait_ge(S_rks, g + 1)
                tt(rko[:], oh[:], rk[:].rearrange("p (t e) -> p t e", e=EXPERTS).unsqueeze(1).broadcast_to([P, 2, G, EXPERTS]),
                   ALU.mult).then_inc(S_ro, 1)

            def position(g):
                dve.wait_ge(S_ro, g + 1)
                ve.tensor_reduce(posf[:], rko[:], X, ALU.add).then_inc(S_pf, 1)

            def int_position(g):
                dve.wait_ge(S_pf, g + 1)
                ve.tensor_copy(posi[:, g % SLOTS], posf[:]).then_inc(S_pi, 1)

            steps = [0]

            def step(ins):
                steps[0] += 1
                ins.then_inc(S_tab, 1)
                dve.wait_ge(S_tab, steps[0])

            def tiles_of(lo, hi):
                n = hi - lo
                wide = [1, n, EXPERTS]
                step(tt(past[:, 0:n], tiota[:, 0:n].unsqueeze(2).broadcast_to(wide), ends[:].unsqueeze(1).broadcast_to(wide), ALU.is_ge))
                ve.tensor_reduce(tef[:, lo:hi], past[:, 0:n, 0:EXPERTS - 1], X, ALU.add)
                step(tt(pstep[:, 0:n], past[:, 0:n], step8[:].unsqueeze(1).broadcast_to(wide), ALU.mult))
                step(ve.tensor_reduce(rowf[:, lo:hi], pstep[:, 0:n, 0:EXPERTS - 1], X, ALU.add))
                step(stt(rowg[:, lo:hi], tiota[:, 0:n], float(P), rowf[:, lo:hi], ALU.mult, ALU.add))

            def words(lo, hi):
                for w in range(WORDS):
                    first = lo * RING + w * DIGITS
                    of_turns = tef[:, first:first + (hi - lo) * RING].rearrange("p (t r) -> p t r", r=RING)
                    last = tt(tew[:, lo:hi, w], of_turns[:, :, 0:DIGITS],
                              pow8[:].unsqueeze(1).broadcast_to([1, hi - lo, DIGITS]), ALU.mult)
                step(last)
                step(ve.tensor_reduce(packf[:, lo:hi], tew[:, lo:hi], X, ALU.add))

            def table_first():
                dve.wait_ge(S_tots, 1)
                step(ve.tensor_copy(totali[:], total[0:1, :]))
                step(ts(nti[:], totali[:], 7, None, ALU.arith_shift_right))
                step(ve.tensor_copy(ntf[:], nti[:]))
                step(ve.tensor_tensor_scan(sums[:], ntf[:], zero8[:], 0.0, ALU.add, ALU.add))
                step(ts(ends[:], sums[:], float(FIRST), None, ALU.min))
                ve.tensor_copy(taken[:, 0:1], ends[:, 0:1])
                step(tt(taken[:, 1:EXPERTS], ends[:, 1:EXPERTS], ends[:, 0:EXPERTS - 1], ALU.subtract))
                step(ts(step8[:], taken[:], -float(P), float(CAP), ALU.mult, ALU.add))
                tiles_of(0, FIRST)
                ve.tensor_copy(rowi[:, 0:FIRST], rowg[:, 0:FIRST])
                words(0, 1)
                ve.tensor_copy(pack[:, 0:1], packf[:, 0:1]).then_inc(S_taba, 1)

            def table_rest(part):
                if part == 0:
                    dve.wait_ge(S_tots, 2)
                    dve.wait_ge(S_taba, 1)
                    ve.tensor_copy(totali[:], total[0:1, :])
                    ts(rowlim[:], total[0:1, EXPERTS - 1:EXPERTS], float((EXPERTS - 1) * CAP), None, ALU.add)
                    ts(start0[:], taken[:, 0:1], float(P), None, ALU.mult)
                    step(ts(ntf[:], total[0:1, :], float(P - 1), None, ALU.add))
                    step(ve.tensor_copy(nti[:], ntf[:]))
                elif part == 1:
                    step(ts(nti[:], nti[:], 7, None, ALU.arith_shift_right))
                    step(ve.tensor_copy(ntf[:], nti[:]))
                    step(tt(left[:], ntf[:], taken[:], ALU.subtract))
                elif part == 2:
                    step(ve.tensor_tensor_scan(ends[:], left[:], zero8[:], 0.0, ALU.add, ALU.add))
                    step(tt(sums[:, 0:EXPERTS - 1], taken[:, 1:EXPERTS], taken[:, 0:EXPERTS - 1], ALU.subtract))
                    step(tt(sums[:, 0:EXPERTS - 1], sums[:, 0:EXPERTS - 1], left[:, 0:EXPERTS - 1], ALU.subtract))
                elif part == 3:
                    step(ts(step8[:, 0:EXPERTS - 1], sums[:, 0:EXPERTS - 1], float(P), float(CAP), ALU.mult, ALU.add))
                elif part == 4:
                    tiles_of(FIRST, LOOKED)
                elif part == 5:
                    ts(rowi[:, FIRST:LOOKED], rowg[:, FIRST:LOOKED], start0[:], rowlim[:], ALU.add, ALU.min)
                    words(1, TURNS)
                elif part == 6:
                    ve.tensor_copy(pack[:, 1:], packf[:, 1:]).then_inc(S_tabd, 1)

            top8(0)
            take8(0)
            for u in range(STEPS):
                if u + 1 < TILES:
                    top8(u + 1)
                if 3 <= u < TILES + 1:
                    tile_stats(u - 3)
                if u < TILES:
                    recip_sum(u)
                if (g := group(u, 7)) is not None:
                    newton1(g)
                if (g := group(u, 8)) is not None:
                    skip_share(g)
                if (g := group(u, 10, LAX)) is not None:
                    name_experts(g)
                if (g := group(u, 12, LAX)) is not None:
                    int_position(g)
                if u + 1 < TILES:
                    take8(u + 1)
                if (g := group(u, 10, LAX)) is not None:
                    float_names(g)
                if 3 <= u < TILES + 1:
                    mean_var(u - 3)
                if (g := group(u, 7)) is not None:
                    newton2(g)
                if (g := group(u, 10, LAX)) is not None:
                    onehots(g)
                if (g := group(u, 11, LAX)) is not None:
                    weight0(g)
                    count_group(g)
                if u < TILES:
                    probs(u)
                if u < 2:
                    basis(CHUNKS - 2 + u, B - 1, u)
                if (g := group(u, 6)) is not None and g < NG - 1:
                    variances(g)
                if (g := group(u, 7)) is not None:
                    newton3(g)
                if (g := group(u, 10, LAX)) is not None:
                    choices(g)
                if (g := group(u, 11, LAX)) is not None:
                    choose_rank(g)
                    weight1(g)
                    add_count(g)
                if 2 <= u < TILES + 1:
                    residual(u - 2)
                if u == TILES:
                    tile_stats(u - 2)
                    residual(u - 1)
                    mean_var(u - 2)
                    tile_stats(u - 1)
                    mean_var(u - 1)
                    variances(NG - 1)
                if (g := group(u, 7)) is not None:
                    scale_and_shift(g)
                if (g := group(u, 9, LAX)) is not None:
                    rank_experts(g)
                if (g := group(u, 10, LAX)) is not None:
                    weight_den(g)
                if (g := group(u, 11, LAX)) is not None:
                    position(g)
                    round_count(g)
                if u == TOTAL_STEP + 1:
                    table_first()

            def hidden(j, r):
                dve.wait_ge(S_si, j + 1)
                dve.wait_ge(S_uu, j + 1)
                tt(hh[:, r % 2, :], PS[:, 1 + r % 2, 0:HIDDEN], sg[:, r % 2, :], ALU.mult).then_inc(S_h, 1)

            def rest_of_rows(j, r):
                dve.wait_ge(S_gs, j + 1)
                if not (isinstance(j, int) and j < 2):
                    dve.wait_ge(S_uu, j - 1)
                tt(xgl[:, r % 2, :], PS[:, 0, 0:P], xgh[:, r % 2, :].bitcast(F32), ALU.subtract).then_inc(S_gl, 1)

            def skips(j, r, turn):
                dve.wait_ge(S_g[r % RING], turn * 16 + 16 * (r // RING) + 16)
                if not (isinstance(j, int) and j < 2):
                    dve.wait_ge(S_yo, j)
                ts(skip[:, r % 2, :], xg[:, r % RING, 0:D], xg[:, r % RING, D + 2:ROW], None, ALU.mult).then_inc(S_ss, 1)

            def weighted(j, r, turn):
                dve.wait_ge(S_dn, j + 1)
                dve.wait_ge(S_ss, j + 1)
                dve.wait_ge(S_g[r], turn * 16 + 16)
                stt(yo[:, r, :], PS[:, 4, 0:D], xg[:, r, D + 1:D + 2], skip[:, r % 2, :], ALU.mult, ALU.add).then_inc(S_yo, 1)

            dve.sem_inc(S_yo, 1)
            skips(0, 0, 0)
            rest_of_rows(0, 0)
            rest_of_rows(1, 1)
            hidden(0, 0)
            rest_of_rows(2, 2)
            hidden(1, 1)

            def tile(j, r, turn, left):
                if left > 3:
                    rest_of_rows(j + 3, r + 3)
                if left > 1:
                    skips(j + 1, r + 1, turn)
                if left > 2:
                    hidden(j + 2, r + 2)
                weighted(j, r, turn)

            for r in range(RING):
                table_rest(r)
                tile(r, r, 0, FTILES)
            with dve.Fori(1, FTILES // RING) as it:
                for r in range(RING):
                    tile(it * RING + r, r, it, FTILES)
            for j in range(WHOLE, FTILES):
                tile(j, j % RING, WHOLE // RING, FTILES - j)

            def final_stats(g):
                dve.wait_ge(S_f1, g + 1)
                for t in range(G):
                    last = ve.bn_stats(st2[:, g % 2, t, :], ya[:, (g * G + t) * D:(g * G + t + 1) * D])
                last.then_inc(S_f3, 1)

            def final_mean(g):
                dve.wait_ge(S_f3, g + 1)
                for t in range(G):
                    last = ve.bn_aggr(mv2[:, g % 2, t, :], st2[:, g % 2, t, :])
                last.then_inc(S_f4, 1)

            def final_var(g):
                dve.wait_ge(S_f4, g + 1)
                ts(vv2[:, g % 2, :], mv2[:, g % 2, :, 1], LN_EPS, None, ALU.add).then_inc(S_l2, 1)

            def final_newton1(g):
                dve.wait_ge(S_f6, g + 1)
                tt(rq2[:, g % 2, :], r02[:, g % 2, :], r02[:, g % 2, :], ALU.mult).then_inc(S_m1, 1)

            def final_newton2(g):
                dve.wait_ge(S_m1, g + 1)
                stt(rh2[:, g % 2, :], rq2[:, g % 2, :], -0.5, vv2[:, g % 2, :], ALU.mult, ALU.mult).then_inc(S_m2, 1)

            def final_newton3(g):
                dve.wait_ge(S_m2, g + 1)
                stt(rs2[:, g % 2, :], rh2[:, g % 2, :], 1.5, r02[:, g % 2, :], ALU.add, ALU.mult).then_inc(S_m3, 1)

            def final_shift(g):
                dve.wait_ge(S_m3, g + 1)
                stt(nm2[:, g % 2, :], mv2[:, g % 2, :, 0], -1.0, rs2[:, g % 2, :], ALU.mult, ALU.mult).then_inc(S_m4, 1)
                if g % 2 == 0:
                    at = slice(g * G * D, (g * G + 1) * D)
                    ts(yb[:, at], ya[:, at], mv2[:, g % 2, 0, 0:1], rs2[:, g % 2, 0:1], ALU.subtract, ALU.mult).then_inc(S_f8, 1)

            for g in range(NG + 1):
                if g < NG:
                    final_stats(g)
                if g >= 1:
                    final_newton1(g - 1)
                if g < NG:
                    final_mean(g)
                if g >= 1:
                    final_newton2(g - 1)
                if g < NG:
                    final_var(g)
                if g >= 1:
                    final_newton3(g - 1)
                    final_shift(g - 1)

        @block.gpsimd
        def _(pool):
            gp = nc.gpsimd
            pool.wait_ge(S_xT[1], 16)
            gp.dma_start(xres[:], io["mu"].rearrange("(t p) n -> p t n", p=P)).then_inc(S_x, 16)

            def sum_window(c, h, projected=None):
                pool.wait_ge(S_sil, c + 1)
                if not (isinstance(c, int) and c == 0):
                    pool.wait_ge(S_loc, c)
                gp.tensor_tensor(sum2, sil[:, 0:2, :], sil[:, 2:4, :], ALU.add).then_inc(S_s2, 1)
                pool.wait_ge(S_s2, c + 1)
                if projected is not None:
                    pool.wait_ge(S_l, projected)
                gp.tensor_tensor(locT[:, h, :], sum2[:, 0, :], sum2[:, 1, :], ALU.add).then_inc(S_loc, 1)

            sum_window(0, 0)
            sum_window(1, 1)
            with pool.Fori(0, B - 1) as b:
                sum_window(b * 2 + 2, 0, b * 2 + 1)
                sum_window(b * 2 + 3, 1, b * 2 + 2)
            pool.wait_ge(S_w, 16 * WLOADS)
            pool.wait_ge(S_c, 16 * CLOADS)
            gp.tensor_scalar(wr[:], wr[:], cols[:, 3:4], 1.0, ALU.mult, ALU.mult).then_inc(S_wrs, 1)
            pool.wait_ge(S_f, 32)
            gp.tensor_scalar(wup[:], wup[:], cols[:, 3:4], 1.0, ALU.mult, ALU.mult).then_inc(S_wsc, 1)
            pool.wait_ge(S_wsc, 1)
            pool.wait_ge(S_l, CHUNKS)
            gp.tensor_copy(wuph, wup[:]).then_inc(S_wsc, 1)
            pool.wait_ge(S_wsc, 2)
            gp.tensor_tensor(wupl, wup[:], wuph.bitcast(F32), ALU.subtract).then_inc(S_wsc, 1)

            pool.wait_ge(S_c, 16 * CLOADS)
            def send(g):
                if g >= SLOTS:
                    pool.wait_ge(S_scat[g % SLOTS], g // SLOTS * (G * 2 * 16))
                gp.tensor_copy(rows[:, g % SLOTS, :, :, D:D + 1].bitcast(I32).rearrange("p t k o -> p t (k o)"),
                               dsts[:, g * G:(g + 1) * G, :]).then_inc(S_ds, 1)
                pool.wait_ge(S_ds, g + 1)
                pool.wait_ge(S_pi, g + 1)
                pool.wait_ge(S_w1, g + 1)
                pool.wait_ge(S_xn, (g + 1) * G)
                pool.wait_ge(S_sk, g + 1)
                for t in range(G):
                    for k in range(2):
                        gp.indirect_dma_start(
                            buckets, bass.IndirectOffsetOnAxis(ap=posi[:, g % SLOTS, k, t:t + 1], axis=0),
                            rows[:, g % SLOTS, t, k, :], None).then_inc(S_scat[g % SLOTS], 16)

            for g in range(NG):
                send(g)

            def scatter(j, r):
                pool.wait_ge(S_yo, j + 2)
                settled(pool)
                gp.indirect_dma_start(
                    ydram, bass.IndirectOffsetOnAxis(ap=xg[:, r, D:D + 1].bitcast(I32), axis=0),
                    yo[:, r, :], None, bounds_check=PAIRS - 1, oob_is_err=False).then_inc(S_ys[r], 16)

            with pool.Fori(0, FTILES // RING) as it:
                for r in range(RING):
                    scatter(it * RING + r, r)
            for j in range(WHOLE, FTILES):
                scatter(j, j % RING)
            for g in range(NG):
                pool.wait_ge(S_ya[g], 32)
                gp.tensor_tensor(ya[:, g * CH:(g + 1) * CH], ya[:, g * CH:(g + 1) * CH], yb[:, g * CH:(g + 1) * CH], ALU.add).then_inc(S_f1, 1)


def kernel(**inputs):
    import ml_dtypes
    import concourse.bacc as bacc
    from concourse.bass_utils import run_bass_kernel_spmd

    g = {k.replace("L0_attn_", "").replace("L0_ffn_", ""): np.asarray(v) for k, v in inputs.items()}
    c = np.ascontiguousarray
    mu = g["mu"].reshape(T, D)
    arrays = {
        "mu": c(mu), "muT": c(mu.T), "Wq": c(g["Wq"]), "Wk": c(g["Wk"]), "Wm1": c(g["Wm1"]), "Wo": c(g["Wo"]),
        "WvT": c(g["Wv"].T), "Wm2T": c(g["Wm2"].T),
        "cols": c(np.stack([g["bq"], g["bk"], g["bm1"], g["norm_scale"]], axis=1)),
        "reps": c(np.stack([np.broadcast_to(g["bm2"][:, None], (D, P)), np.broadcast_to(g["bv"][:, None], (D, P)),
                            np.broadcast_to(g["bo"][None, :], (P, D))], axis=1)),
        "wrT": c(g["w_router"].T),
        "wupT": c(g["w_up"].transpose(2, 0, 1).reshape(D, EXPERTS * 2 * HIDDEN)),
        "wdnT": c(g["w_down"].transpose(2, 0, 1).reshape(2, P, EXPERTS, D).transpose(1, 2, 0, 3).reshape(P, EXPERTS * HIDDEN)),
    }
    r = np.arange(P)
    arrays["ident"] = np.eye(P, dtype=np.float32)
    arrays["cbf"] = np.stack([np.eye(P), np.where(r[None, :] > r[:, None], MASKED, 0.0),
                              r[:, None] < r[None, :], np.ones((P, P))], axis=1).astype(ml_dtypes.bfloat16)
    arrays["ebase"] = np.broadcast_to(np.tile(np.arange(EXPERTS) * CAP, G), (P, G * EXPERTS)).astype(ml_dtypes.bfloat16)
    arrays["iota8"] = np.broadcast_to(np.arange(EXPERTS, dtype=np.float32), (P, EXPERTS)).copy()
    tile = np.array([seq * BT + i for seq, i in ORDER])
    arrays["dsts"] = (r[:, None, None] * G + (tile // G * G * P + tile % G)[None, :, None] + np.arange(2)[None, None, :] * T).astype(np.int32)
    arrays["tiota"] = np.arange(TABLE, dtype=np.float32)[None, :]
    arrays["pow8"] = (float(EXPERTS) ** np.arange(DIGITS, dtype=np.float32))[None, :].astype(np.float32)
    arrays["epsc"] = np.broadcast_to(np.array([LN_EPS, RMS_EPS * LN_EPS], np.float32), (P, 2)).copy()

    nc = bacc.Bacc("TRN2", target_bir_lowering=False, num_devices=1)
    io = {k: nc.dram_tensor(f"in_{k}", a.shape, mybir.dt.from_np(a.dtype), kind="ExternalInput").ap() for k, a in arrays.items()}
    io["out"] = nc.dram_tensor("out", [T, D], mybir.dt.float32, kind="ExternalOutput").ap()
    build(nc, io)
    res = run_bass_kernel_spmd(nc, [{f"in_{k}": a for k, a in arrays.items()}], core_ids=[0])
    return res.results[0]["out"].reshape(B, N, D)
```
